# Optimizing a Trainium2 kernel written in Bass

```python
import numpy as np
import jax
import jax.numpy as jnp

def _softmax(x, axis=-1):
    return jax.nn.softmax(x, axis=axis)

def _gelu(x):
    return jax.nn.gelu(x, approximate=True)

def _silu(x):
    return jax.nn.silu(x)

def _sigmoid(x):
    return jax.nn.sigmoid(x)

def _layernorm(x, axis=-1, eps=1e-05):
    m = jnp.mean(x, axis=axis, keepdims=True)
    v = jnp.var(x, axis=axis, keepdims=True)
    return (x - m) / jnp.sqrt(v + eps)

def _scatter_add(tgt, idx, src, axis=0):
    return tgt.at[idx].add(src)

def _segment_sum(src, seg, n):
    return jax.ops.segment_sum(src, seg, n)
kernel_name = 'mk_hybrid_d2_jaxref_r4_1bf1d2'

def setup_inputs(seed: int=0):
    np.random.seed(seed)
    _w = jnp.asarray

    def _L0_attn_a_setup():
        import jax, jax.numpy as jnp
        import numpy as np
        import math
        N_HEAD = 8
        N_EMBD = 256
        HEAD_DIM = N_EMBD // N_HEAD // 2
        LAYER_IDX = 4
        LAMBDA_INIT = 0.8 - 0.6 * math.exp(-0.3 * LAYER_IDX)
        RMS_EPS = float(jnp.finfo(jnp.float32).eps)
        LN_EPS = 1e-05

        def rmsnorm(x):
            return x * jax.lax.rsqrt(jnp.mean(x * x, axis=-1, keepdims=True) + RMS_EPS)

        def layernorm(x):
            mu = jnp.mean(x, axis=-1, keepdims=True)
            var = jnp.mean(jnp.square(x - mu), axis=-1, keepdims=True)
            return (x - mu) * jax.lax.rsqrt(var + LN_EPS)

        def rope_tables(T, dim, dtype):
            inv_freq = 1.0 / 10000.0 ** (np.arange(0, dim, 2, dtype=np.float32) / dim)
            t = np.arange(T, dtype=np.float32)
            freqs = np.outer(t, inv_freq)
            return (jnp.asarray(np.cos(freqs), dtype), jnp.asarray(np.sin(freqs), dtype))

        def apply_rotary(x, cos, sin):
            d = x.shape[-1] // 2
            x1, x2 = (x[..., :d], x[..., d:])
            c = cos[None, :, None, :]
            s = sin[None, :, None, :]
            return jnp.concatenate([x1 * c + x2 * s, -x1 * s + x2 * c], axis=-1)
        key = jax.random.key(seed)
        ks = jax.random.split(key, 9)
        B, T, C = (4, 512, N_EMBD)
        scale = 1.0 / math.sqrt(C)
        return {'x': jax.random.normal(ks[0], (B, T, C), jnp.float32), 'Wq': jax.random.normal(ks[1], (C, C), jnp.float32) * scale, 'Wk': jax.random.normal(ks[2], (C, C), jnp.float32) * scale, 'Wv': jax.random.normal(ks[3], (C, C), jnp.float32) * scale, 'Wproj': jax.random.normal(ks[4], (C, C), jnp.float32) * scale, 'lq1': jax.random.normal(ks[5], (HEAD_DIM,), jnp.float32) * 0.1, 'lk1': jax.random.normal(ks[6], (HEAD_DIM,), jnp.float32) * 0.1, 'lq2': jax.random.normal(ks[7], (HEAD_DIM,), jnp.float32) * 0.1, 'lk2': jax.random.normal(ks[8], (HEAD_DIM,), jnp.float32) * 0.1}
    _L0_attn_a_in = _L0_attn_a_setup()

    def _L0_attn_b_setup():
        import jax, jax.numpy as jnp
        import numpy as np
        B, N, D = (2, 1024, 256)
        H, Dh = (8, 64)
        INNER = H * Dh
        W = 64
        NQ = NKV = 256

        def _forward(x, gamma_h, wq_h, wkv_h, wo_h, ln_g, ln_b, wqkv_l, wo_l, rt_q, rt_kv):
            b, n, d = x.shape
            scale = Dh ** (-0.5)
            neg = -jnp.finfo(x.dtype).max
            mu = jnp.mean(x, -1, keepdims=True)
            var = jnp.var(x, -1, keepdims=True)
            xl = (x - mu) / jnp.sqrt(var + 1e-05) * ln_g + ln_b
            q, k, v = jnp.split(xl @ wqkv_l, 3, -1)

            def heads(t):
                return t.reshape(b, n, H, Dh).transpose(0, 2, 1, 3)
            q, k, v = (heads(q), heads(k), heads(v))
            nw = n // W
            qw = q.reshape(b, H, nw, W, Dh)

            def look_around(t):
                tw = t.reshape(b, H, nw, W, Dh)
                tp = jnp.pad(tw, ((0, 0), (0, 0), (1, 1), (0, 0), (0, 0)))
                return jnp.concatenate([tp[:, :, s:s + nw] for s in range(3)], axis=3)
            kk, vv = (look_around(k), look_around(v))
            wi = jnp.arange(nw)[:, None]
            sh = jnp.arange(3)[None, :]
            valid = (wi + sh - 1 >= 0) & (wi + sh - 1 < nw)
            valid = jnp.repeat(valid, W, axis=1)
            sim = jnp.einsum('bhnid,bhnjd->bhnij', qw * scale, kk)
            sim = jnp.where(valid[None, None, :, None, :], sim, neg)
            attn = jax.nn.softmax(sim, axis=-1)
            lo = jnp.einsum('bhnij,bhnjd->bhnid', attn, vv)
            light_out = lo.reshape(b, H, n, Dh).transpose(0, 2, 1, 3).reshape(b, n, INNER) @ wo_l

            def route(rt, num):
                scores = jnp.einsum('bnd,d->bn', x, rt)
                idx = jnp.argsort(scores, axis=-1)
                s = jnp.take_along_axis(scores, idx, -1)
                s = s - jax.lax.stop_gradient(jnp.max(s, -1, keepdims=True))
                e = jnp.exp(s)
                cs = e / jnp.clip(jnp.cumsum(e, -1), 1e-06, None)
                sel_s, sel_i = (cs[:, -num:], idx[:, -num:])
                sel_s = sel_s + jax.lax.stop_gradient(1.0 - sel_s)
                return (sel_s, sel_i)
            sq, iq = route(rt_q, NQ)
            skv, ikv = route(rt_kv, NKV)
            rq = jnp.take_along_axis(x, iq[:, :, None], 1)
            rkv = jnp.take_along_axis(x, ikv[:, :, None], 1)

            def rms(t):
                t = t / jnp.clip(jnp.linalg.norm(t, axis=-1, keepdims=True), 1e-12, None)
                return t * d ** 0.5 * gamma_h
            hq = (rms(rq) @ wq_h).reshape(b, NQ, H, Dh).transpose(0, 2, 1, 3)
            hk, hv = jnp.split(rms(rkv) @ wkv_h, 2, -1)
            hk = hk.reshape(b, NKV, H, Dh).transpose(0, 2, 1, 3)
            hv = hv.reshape(b, NKV, H, Dh).transpose(0, 2, 1, 3)
            hv = hv * skv[:, None, :, None]
            hsim = jnp.einsum('bhid,bhjd->bhij', hq * scale, hk)
            hattn = jax.nn.softmax(hsim, axis=-1)
            ho = jnp.einsum('bhij,bhjd->bhid', hattn, hv)
            ho = ho.transpose(0, 2, 1, 3).reshape(b, NQ, INNER) @ wo_h
            ho = ho * sq[:, :, None]
            heavy_out = jnp.zeros_like(x).at[jnp.arange(b)[:, None], iq].set(ho)
            return light_out + heavy_out
        key = jax.random.key(seed)
        ks = jax.random.split(key, 8)
        std = 0.02
        return {'x': jax.random.normal(ks[0], (B, N, D), jnp.float32), 'gamma_h': jnp.ones((D,), jnp.float32), 'wq_h': jax.random.normal(ks[1], (D, INNER), jnp.float32) * std, 'wkv_h': jax.random.normal(ks[2], (D, 2 * INNER), jnp.float32) * std, 'wo_h': jax.random.normal(ks[3], (INNER, D), jnp.float32) * std, 'ln_g': jnp.ones((D,), jnp.float32), 'ln_b': jnp.zeros((D,), jnp.float32), 'wqkv_l': jax.random.normal(ks[4], (D, 3 * INNER), jnp.float32) * std, 'wo_l': jax.random.normal(ks[5], (INNER, D), jnp.float32) * std, 'rt_q': jax.random.normal(ks[6], (D,), jnp.float32), 'rt_kv': jax.random.normal(ks[7], (D,), jnp.float32)}
    _L0_attn_b_in = _L0_attn_b_setup()

    def _L0_ffn_setup():
        import jax, jax.numpy as jnp
        import numpy as np
        D = 256
        H = 512
        E = 8
        TOP_K = 2
        N_SHARED = 1
        B, S = (2, 256)
        key = jax.random.key(seed)
        ks = jax.random.split(key, 12)
        sc = 0.02
        return {'hidden': jax.random.normal(ks[0], (B, S, D), jnp.float32), 'router_w': jax.random.normal(ks[1], (D, E), jnp.float32) * sc, 'router_b': jnp.zeros((E,), jnp.float32), 'sw1': jax.random.normal(ks[2], (D, H), jnp.float32) * sc, 'sb1': jnp.zeros((H,), jnp.float32), 'sw2': jax.random.normal(ks[3], (H, D), jnp.float32) * sc, 'sb2': jnp.zeros((D,), jnp.float32), 'rw1': jax.random.normal(ks[4], (E, D, H), jnp.float32) * sc, 'rb1': jnp.zeros((E, H), jnp.float32), 'rw2': jax.random.normal(ks[5], (E, H, D), jnp.float32) * sc, 'rb2': jnp.zeros((E, D), jnp.float32)}
    _L0_ffn_in = _L0_ffn_setup()

    def _L1_attn_a_setup():
        import jax, jax.numpy as jnp
        import numpy as np
        D_MODEL, D_STATE, D_CONV, EXPAND = (256, 16, 4, 2)
        D_INNER = EXPAND * D_MODEL
        BATCH, SEQ = (4, 512)
        key = jax.random.key(seed)
        ks = jax.random.split(key, 10)
        s_in = 1.0 / np.sqrt(D_MODEL)
        s_x = 1.0 / np.sqrt(D_INNER)
        return {'x': jax.random.normal(ks[0], (BATCH, SEQ, D_MODEL), jnp.float32), 'W_in': jax.random.normal(ks[1], (2 * D_INNER, D_MODEL), jnp.float32) * s_in, 'conv_w': jax.random.normal(ks[2], (D_INNER, 1, D_CONV), jnp.float32) * 0.5, 'conv_b': jax.random.normal(ks[3], (D_INNER,), jnp.float32) * 0.1, 'W_x': jax.random.normal(ks[4], (2 * D_STATE, D_INNER), jnp.float32) * s_x, 'W_dt': jax.random.normal(ks[5], (D_STATE, D_INNER), jnp.float32) * s_x, 'b_dt': jax.random.normal(ks[6], (D_STATE,), jnp.float32) * 0.1, 'A_log': jax.random.normal(ks[7], (D_STATE,), jnp.float32), 'D': jnp.ones((D_INNER,), jnp.float32), 'W_out': jax.random.normal(ks[8], (D_MODEL, D_INNER), jnp.float32) * s_x}
    _L1_attn_a_in = _L1_attn_a_setup()

    def _L1_attn_b_setup():
        import jax, jax.numpy as jnp
        import numpy as np
        EMBED = 256
        HEADS = 16
        HEAD_DIM = EMBED // HEADS
        B, T = (2, 512)
        ROPE_THETA = 10000.0

        def _rope(x):
            D = x.shape[-1]
            inv_freq = 1.0 / ROPE_THETA ** (jnp.arange(0, D, 2, dtype=jnp.float32) / D)
            freqs = jnp.arange(x.shape[2], dtype=jnp.float32)[:, None] * inv_freq[None, :]
            cos = jnp.cos(freqs).astype(x.dtype)
            sin = jnp.sin(freqs).astype(x.dtype)
            x1, x2 = (x[..., :D // 2], x[..., D // 2:])
            return jnp.concatenate([x1 * cos - x2 * sin, x2 * cos + x1 * sin], axis=-1)
        key = jax.random.key(seed)
        ks = jax.random.split(key, 5)
        s = 1.0 / np.sqrt(EMBED)
        return {'x': jax.random.normal(ks[0], (B, T, EMBED), dtype=jnp.float32), 'Wq': jax.random.normal(ks[1], (EMBED, EMBED), dtype=jnp.float32) * s, 'bq': jnp.zeros((EMBED,), dtype=jnp.float32), 'Wk': jax.random.normal(ks[2], (EMBED, EMBED), dtype=jnp.float32) * s, 'bk': jnp.zeros((EMBED,), dtype=jnp.float32), 'Wv': jax.random.normal(ks[3], (EMBED, EMBED), dtype=jnp.float32) * s, 'bv': jnp.zeros((EMBED,), dtype=jnp.float32), 'Wo': jax.random.normal(ks[4], (EMBED, EMBED), dtype=jnp.float32) * s, 'bo': jnp.zeros((EMBED,), dtype=jnp.float32)}
    _L1_attn_b_in = _L1_attn_b_setup()

    def _L1_ffn_setup():
        import jax, jax.numpy as jnp
        import numpy as np
        BLOCK = 16
        _GRID = jnp.array([0.0, 0.5, 1.0, 1.5, 2.0, 3.0, 4.0, 6.0], dtype=jnp.float32)
        _MID = jnp.array([0.25, 0.75, 1.25, 1.75, 2.5, 3.5, 5.0], dtype=jnp.float32)

        def fp4_quant_dequant(x):
            shape = x.shape
            xb = x.reshape(shape[:-1] + (shape[-1] // BLOCK, BLOCK))
            scale = jnp.max(jnp.abs(xb), axis=-1, keepdims=True) / 6.0
            scale = jnp.maximum(scale, jnp.float32(1e-12))
            xn = xb / scale
            idx = jnp.searchsorted(_MID, jnp.abs(xn))
            q = _GRID[idx] * jnp.sign(xn) * scale
            return q.reshape(shape)

        def fp4_linear(x, w):
            xq = fp4_quant_dequant(x)
            wq = fp4_quant_dequant(w)
            return jnp.einsum('bsk,nk->bsn', xq, wq)
        key = jax.random.key(seed)
        k1, k2, k3, k4 = jax.random.split(key, 4)
        H, I = (256, 704)
        x = jax.random.normal(k1, (4, 1024, H), dtype=jnp.float32)
        w_gate = jax.random.normal(k2, (I, H), dtype=jnp.float32) * 0.02
        w_up = jax.random.normal(k3, (I, H), dtype=jnp.float32) * 0.02
        w_down = jax.random.normal(k4, (H, I), dtype=jnp.float32) * 0.02
        return {'x': x, 'w_gate': w_gate, 'w_up': w_up, 'w_down': w_down}
    _L1_ffn_in = _L1_ffn_setup()
    _d = {'L0_attn_a_x': _L0_attn_a_in['x'], 'L0_attn_a_Wq': _L0_attn_a_in['Wq'], 'L0_attn_a_Wk': _L0_attn_a_in['Wk'], 'L0_attn_a_Wv': _L0_attn_a_in['Wv'], 'L0_attn_a_Wproj': _L0_attn_a_in['Wproj'], 'L0_attn_a_lq1': _L0_attn_a_in['lq1'], 'L0_attn_a_lk1': _L0_attn_a_in['lk1'], 'L0_attn_a_lq2': _L0_attn_a_in['lq2'], 'L0_attn_a_lk2': _L0_attn_a_in['lk2'], 'L0_attn_b_gamma_h': _L0_attn_b_in['gamma_h'], 'L0_attn_b_wq_h': _L0_attn_b_in['wq_h'], 'L0_attn_b_wkv_h': _L0_attn_b_in['wkv_h'], 'L0_attn_b_wo_h': _L0_attn_b_in['wo_h'], 'L0_attn_b_ln_g': _L0_attn_b_in['ln_g'], 'L0_attn_b_ln_b': _L0_attn_b_in['ln_b'], 'L0_attn_b_wqkv_l': _L0_attn_b_in['wqkv_l'], 'L0_attn_b_wo_l': _L0_attn_b_in['wo_l'], 'L0_attn_b_rt_q': _L0_attn_b_in['rt_q'], 'L0_attn_b_rt_kv': _L0_attn_b_in['rt_kv'], 'L0_ffn_router_w': _L0_ffn_in['router_w'], 'L0_ffn_router_b': _L0_ffn_in['router_b'], 'L0_ffn_sw1': _L0_ffn_in['sw1'], 'L0_ffn_sb1': _L0_ffn_in['sb1'], 'L0_ffn_sw2': _L0_ffn_in['sw2'], 'L0_ffn_sb2': _L0_ffn_in['sb2'], 'L0_ffn_rw1': _L0_ffn_in['rw1'], 'L0_ffn_rb1': _L0_ffn_in['rb1'], 'L0_ffn_rw2': _L0_ffn_in['rw2'], 'L0_ffn_rb2': _L0_ffn_in['rb2'], 'L1_attn_a_W_in': _L1_attn_a_in['W_in'], 'L1_attn_a_conv_w': _L1_attn_a_in['conv_w'], 'L1_attn_a_conv_b': _L1_attn_a_in['conv_b'], 'L1_attn_a_W_x': _L1_attn_a_in['W_x'], 'L1_attn_a_W_dt': _L1_attn_a_in['W_dt'], 'L1_attn_a_b_dt': _L1_attn_a_in['b_dt'], 'L1_attn_a_A_log': _L1_attn_a_in['A_log'], 'L1_attn_a_D': _L1_attn_a_in['D'], 'L1_attn_a_W_out': _L1_attn_a_in['W_out'], 'L1_attn_b_Wq': _L1_attn_b_in['Wq'], 'L1_attn_b_bq': _L1_attn_b_in['bq'], 'L1_attn_b_Wk': _L1_attn_b_in['Wk'], 'L1_attn_b_bk': _L1_attn_b_in['bk'], 'L1_attn_b_Wv': _L1_attn_b_in['Wv'], 'L1_attn_b_bv': _L1_attn_b_in['bv'], 'L1_attn_b_Wo': _L1_attn_b_in['Wo'], 'L1_attn_b_bo': _L1_attn_b_in['bo'], 'L1_ffn_w_gate': _L1_ffn_in['w_gate'], 'L1_ffn_w_up': _L1_ffn_in['w_up'], 'L1_ffn_w_down': _L1_ffn_in['w_down']}
    _x0 = _d['L0_attn_a_x']
    _d['L0_attn_a_x'] = jax.random.normal(jax.random.fold_in(jax.random.key(seed), 1), (8, 512, 256), dtype=_x0.dtype)
    del _x0
    return _d

def reference(L0_attn_a_x, L0_attn_a_Wq, L0_attn_a_Wk, L0_attn_a_Wv, L0_attn_a_Wproj, L0_attn_a_lq1, L0_attn_a_lk1, L0_attn_a_lq2, L0_attn_a_lk2, L0_attn_b_gamma_h, L0_attn_b_wq_h, L0_attn_b_wkv_h, L0_attn_b_wo_h, L0_attn_b_ln_g, L0_attn_b_ln_b, L0_attn_b_wqkv_l, L0_attn_b_wo_l, L0_attn_b_rt_q, L0_attn_b_rt_kv, L0_ffn_router_w, L0_ffn_router_b, L0_ffn_sw1, L0_ffn_sb1, L0_ffn_sw2, L0_ffn_sb2, L0_ffn_rw1, L0_ffn_rb1, L0_ffn_rw2, L0_ffn_rb2, L1_attn_a_W_in, L1_attn_a_conv_w, L1_attn_a_conv_b, L1_attn_a_W_x, L1_attn_a_W_dt, L1_attn_a_b_dt, L1_attn_a_A_log, L1_attn_a_D, L1_attn_a_W_out, L1_attn_b_Wq, L1_attn_b_bq, L1_attn_b_Wk, L1_attn_b_bk, L1_attn_b_Wv, L1_attn_b_bv, L1_attn_b_Wo, L1_attn_b_bo, L1_ffn_w_gate, L1_ffn_w_up, L1_ffn_w_down):

    def _L0_attn_a_ref(x, Wq, Wk, Wv, Wproj, lq1, lk1, lq2, lk2):
        import jax, jax.numpy as jnp
        import numpy as np
        import math
        N_HEAD = 8
        N_EMBD = 256
        HEAD_DIM = N_EMBD // N_HEAD // 2
        LAYER_IDX = 4
        LAMBDA_INIT = 0.8 - 0.6 * math.exp(-0.3 * LAYER_IDX)
        RMS_EPS = float(jnp.finfo(jnp.float32).eps)
        LN_EPS = 1e-05

        def rmsnorm(x):
            return x * jax.lax.rsqrt(jnp.mean(x * x, axis=-1, keepdims=True) + RMS_EPS)

        def layernorm(x):
            mu = jnp.mean(x, axis=-1, keepdims=True)
            var = jnp.mean(jnp.square(x - mu), axis=-1, keepdims=True)
            return (x - mu) * jax.lax.rsqrt(var + LN_EPS)

        def rope_tables(T, dim, dtype):
            inv_freq = 1.0 / 10000.0 ** (np.arange(0, dim, 2, dtype=np.float32) / dim)
            t = np.arange(T, dtype=np.float32)
            freqs = np.outer(t, inv_freq)
            return (jnp.asarray(np.cos(freqs), dtype), jnp.asarray(np.sin(freqs), dtype))

        def apply_rotary(x, cos, sin):
            d = x.shape[-1] // 2
            x1, x2 = (x[..., :d], x[..., d:])
            c = cos[None, :, None, :]
            s = sin[None, :, None, :]
            return jnp.concatenate([x1 * c + x2 * s, -x1 * s + x2 * c], axis=-1)
        B, T, C = x.shape
        H, hd = (N_HEAD, HEAD_DIM)
        q = (x @ Wq.T).reshape(B, T, 2 * H, hd)
        k = (x @ Wk.T).reshape(B, T, 2 * H, hd)
        v = (x @ Wv.T).reshape(B, T, H, 2 * hd)
        cos, sin = rope_tables(T, hd, x.dtype)
        q = apply_rotary(rmsnorm(q), cos, sin)
        k = apply_rotary(rmsnorm(k), cos, sin)
        q = jnp.transpose(q, (0, 2, 1, 3)) * (1.0 / math.sqrt(hd))
        k = jnp.transpose(k, (0, 2, 1, 3))
        v = jnp.transpose(v, (0, 2, 1, 3))
        scores = jnp.einsum('bhqd,bhkd->bhqk', q, k)
        causal = jnp.tril(jnp.ones((T, T), bool))
        scores = jnp.where(causal[None, None], scores, -jnp.inf)
        attn = jax.nn.softmax(scores.astype(jnp.float32), axis=-1).astype(scores.dtype)
        attn = attn.reshape(B, H, 2, T, T)
        lam1 = jnp.exp(jnp.sum(lq1 * lk1))
        lam2 = jnp.exp(jnp.sum(lq2 * lk2))
        lam = lam1 - lam2 + LAMBDA_INIT
        attn = attn[:, :, 0] - lam * attn[:, :, 1]
        out = jnp.einsum('bhqk,bhkd->bhqd', attn, v)
        out = layernorm(out) * (1.0 - LAMBDA_INIT)
        out = jnp.transpose(out, (0, 2, 1, 3)).reshape(B, T, C)
        return out @ Wproj.T

    def _L0_attn_b_ref(x, gamma_h, wq_h, wkv_h, wo_h, ln_g, ln_b, wqkv_l, wo_l, rt_q, rt_kv):
        import jax, jax.numpy as jnp
        import numpy as np
        B, N, D = (2, 1024, 256)
        H, Dh = (8, 64)
        INNER = H * Dh
        W = 64
        NQ = NKV = 256

        def _forward(x, gamma_h, wq_h, wkv_h, wo_h, ln_g, ln_b, wqkv_l, wo_l, rt_q, rt_kv):
            b, n, d = x.shape
            scale = Dh ** (-0.5)
            neg = -jnp.finfo(x.dtype).max
            mu = jnp.mean(x, -1, keepdims=True)
            var = jnp.var(x, -1, keepdims=True)
            xl = (x - mu) / jnp.sqrt(var + 1e-05) * ln_g + ln_b
            q, k, v = jnp.split(xl @ wqkv_l, 3, -1)

            def heads(t):
                return t.reshape(b, n, H, Dh).transpose(0, 2, 1, 3)
            q, k, v = (heads(q), heads(k), heads(v))
            nw = n // W
            qw = q.reshape(b, H, nw, W, Dh)

            def look_around(t):
                tw = t.reshape(b, H, nw, W, Dh)
                tp = jnp.pad(tw, ((0, 0), (0, 0), (1, 1), (0, 0), (0, 0)))
                return jnp.concatenate([tp[:, :, s:s + nw] for s in range(3)], axis=3)
            kk, vv = (look_around(k), look_around(v))
            wi = jnp.arange(nw)[:, None]
            sh = jnp.arange(3)[None, :]
            valid = (wi + sh - 1 >= 0) & (wi + sh - 1 < nw)
            valid = jnp.repeat(valid, W, axis=1)
            sim = jnp.einsum('bhnid,bhnjd->bhnij', qw * scale, kk)
            sim = jnp.where(valid[None, None, :, None, :], sim, neg)
            attn = jax.nn.softmax(sim, axis=-1)
            lo = jnp.einsum('bhnij,bhnjd->bhnid', attn, vv)
            light_out = lo.reshape(b, H, n, Dh).transpose(0, 2, 1, 3).reshape(b, n, INNER) @ wo_l

            def route(rt, num):
                scores = jnp.einsum('bnd,d->bn', x, rt)
                idx = jnp.argsort(scores, axis=-1)
                s = jnp.take_along_axis(scores, idx, -1)
                s = s - jax.lax.stop_gradient(jnp.max(s, -1, keepdims=True))
                e = jnp.exp(s)
                cs = e / jnp.clip(jnp.cumsum(e, -1), 1e-06, None)
                sel_s, sel_i = (cs[:, -num:], idx[:, -num:])
                sel_s = sel_s + jax.lax.stop_gradient(1.0 - sel_s)
                return (sel_s, sel_i)
            sq, iq = route(rt_q, NQ)
            skv, ikv = route(rt_kv, NKV)
            rq = jnp.take_along_axis(x, iq[:, :, None], 1)
            rkv = jnp.take_along_axis(x, ikv[:, :, None], 1)

            def rms(t):
                t = t / jnp.clip(jnp.linalg.norm(t, axis=-1, keepdims=True), 1e-12, None)
                return t * d ** 0.5 * gamma_h
            hq = (rms(rq) @ wq_h).reshape(b, NQ, H, Dh).transpose(0, 2, 1, 3)
            hk, hv = jnp.split(rms(rkv) @ wkv_h, 2, -1)
            hk = hk.reshape(b, NKV, H, Dh).transpose(0, 2, 1, 3)
            hv = hv.reshape(b, NKV, H, Dh).transpose(0, 2, 1, 3)
            hv = hv * skv[:, None, :, None]
            hsim = jnp.einsum('bhid,bhjd->bhij', hq * scale, hk)
            hattn = jax.nn.softmax(hsim, axis=-1)
            ho = jnp.einsum('bhij,bhjd->bhid', hattn, hv)
            ho = ho.transpose(0, 2, 1, 3).reshape(b, NQ, INNER) @ wo_h
            ho = ho * sq[:, :, None]
            heavy_out = jnp.zeros_like(x).at[jnp.arange(b)[:, None], iq].set(ho)
            return light_out + heavy_out
        return _forward(x, gamma_h, wq_h, wkv_h, wo_h, ln_g, ln_b, wqkv_l, wo_l, rt_q, rt_kv)

    def _L0_ffn_ref(hidden, router_w, router_b, sw1, sb1, sw2, sb2, rw1, rb1, rw2, rb2):
        import jax, jax.numpy as jnp
        import numpy as np
        D = 256
        H = 512
        E = 8
        TOP_K = 2
        N_SHARED = 1
        B, S = (2, 256)
        b, s, d = hidden.shape
        T = b * s
        flat = hidden.reshape(T, d)
        router_logits = flat @ router_w + router_b
        router_probs = jax.nn.softmax(router_logits, axis=-1)
        topk_probs, topk_idx = jax.lax.top_k(router_probs, TOP_K)
        weights = jnp.zeros_like(router_probs).at[jnp.arange(T)[:, None], topk_idx].add(topk_probs)
        sh = jax.nn.gelu(flat @ sw1 + sb1, approximate=False)
        shared_out = (sh @ sw2 + sb2) / N_SHARED
        h1 = jax.nn.gelu(jnp.einsum('td,edh->teh', flat, rw1) + rb1[None], approximate=False)
        expert_out = jnp.einsum('teh,ehd->ted', h1, rw2) + rb2[None]
        mixed = jnp.einsum('ted,te->td', expert_out, weights)
        return (shared_out + mixed).reshape(b, s, d)

    def _L1_attn_a_ref(x, W_in, conv_w, conv_b, W_x, W_dt, b_dt, A_log, D, W_out):
        import jax, jax.numpy as jnp
        import numpy as np
        D_MODEL, D_STATE, D_CONV, EXPAND = (256, 16, 4, 2)
        D_INNER = EXPAND * D_MODEL
        BATCH, SEQ = (4, 512)
        B, L, _ = x.shape
        d_inner = conv_w.shape[0]
        d_conv = conv_w.shape[-1]
        n = A_log.shape[0]
        xz = x @ W_in.T
        xi, z = jnp.split(xz, 2, axis=-1)
        xc = jnp.transpose(xi, (0, 2, 1))
        xc = jax.lax.conv_general_dilated(xc, conv_w, window_strides=(1,), padding=[(d_conv - 1, 0)], feature_group_count=d_inner, dimension_numbers=('NCH', 'OIH', 'NCH'))
        xc = xc + conv_b[None, :, None]
        u = jax.nn.silu(jnp.transpose(xc, (0, 2, 1)))
        bc = u @ W_x.T
        Bm, Cm = jnp.split(bc, 2, axis=-1)
        delta = jax.nn.softplus(u @ W_dt.T + b_dt)
        A = -jnp.exp(A_log)
        dA = jnp.exp(delta * A)
        dB = delta * Bm

        def step(h, inp):
            dA_t, dB_t, u_t, c_t = inp
            h = dA_t[:, None, :] * h + u_t[:, :, None] * dB_t[:, None, :]
            y = jnp.einsum('ben,bn->be', h, c_t)
            return (h, y)
        h0 = jnp.zeros((B, d_inner, n), x.dtype)
        xs = (jnp.swapaxes(dA, 0, 1), jnp.swapaxes(dB, 0, 1), jnp.swapaxes(u, 0, 1), jnp.swapaxes(Cm, 0, 1))
        _, ys = jax.lax.scan(step, h0, xs)
        y = jnp.swapaxes(ys, 0, 1) + u * D
        y = y * jax.nn.silu(z)
        return y @ W_out.T

    def _L1_attn_b_ref(x, Wq, bq, Wk, bk, Wv, bv, Wo, bo):
        import jax, jax.numpy as jnp
        import numpy as np
        EMBED = 256
        HEADS = 16
        HEAD_DIM = EMBED // HEADS
        B, T = (2, 512)
        ROPE_THETA = 10000.0

        def _rope(x):
            D = x.shape[-1]
            inv_freq = 1.0 / ROPE_THETA ** (jnp.arange(0, D, 2, dtype=jnp.float32) / D)
            freqs = jnp.arange(x.shape[2], dtype=jnp.float32)[:, None] * inv_freq[None, :]
            cos = jnp.cos(freqs).astype(x.dtype)
            sin = jnp.sin(freqs).astype(x.dtype)
            x1, x2 = (x[..., :D // 2], x[..., D // 2:])
            return jnp.concatenate([x1 * cos - x2 * sin, x2 * cos + x1 * sin], axis=-1)
        Bb, Tt, C = x.shape
        H, D = (HEADS, HEAD_DIM)

        def proj(W, b):
            return (jnp.einsum('btc,oc->bto', x, W) + b).reshape(Bb, Tt, H, D).transpose(0, 2, 1, 3)
        q = _rope(proj(Wq, bq))
        k = _rope(proj(Wk, bk))
        v = proj(Wv, bv)
        scale = jnp.sqrt(jnp.asarray(D, dtype=x.dtype))
        scores = jnp.einsum('bhtd,bhsd->bhts', q, k) / scale
        attn = jax.nn.softmax(scores, axis=-1)
        out = jnp.einsum('bhts,bhsd->bhtd', attn, v)
        out = out.transpose(0, 2, 1, 3).reshape(Bb, Tt, C)
        return jnp.einsum('btc,oc->bto', out, Wo) + bo

    def _L1_ffn_ref(x, w_gate, w_up, w_down):
        import jax, jax.numpy as jnp
        import numpy as np
        BLOCK = 16
        _GRID = jnp.array([0.0, 0.5, 1.0, 1.5, 2.0, 3.0, 4.0, 6.0], dtype=jnp.float32)
        _MID = jnp.array([0.25, 0.75, 1.25, 1.75, 2.5, 3.5, 5.0], dtype=jnp.float32)

        def fp4_quant_dequant(x):
            shape = x.shape
            xb = x.reshape(shape[:-1] + (shape[-1] // BLOCK, BLOCK))
            scale = jnp.max(jnp.abs(xb), axis=-1, keepdims=True) / 6.0
            scale = jnp.maximum(scale, jnp.float32(1e-12))
            xn = xb / scale
            idx = jnp.searchsorted(_MID, jnp.abs(xn))
            q = _GRID[idx] * jnp.sign(xn) * scale
            return q.reshape(shape)

        def fp4_linear(x, w):
            xq = fp4_quant_dequant(x)
            wq = fp4_quant_dequant(w)
            return jnp.einsum('bsk,nk->bsn', xq, wq)
        gate = fp4_linear(x, w_gate)
        y = fp4_linear(x, w_up)
        h = jax.nn.silu(gate) * y
        return fp4_linear(h, w_down)
    x = L0_attn_a_x
    x = x + _L0_attn_a_ref(_layernorm(x, axis=-1), L0_attn_a_Wq, L0_attn_a_Wk, L0_attn_a_Wv, L0_attn_a_Wproj, L0_attn_a_lq1, L0_attn_a_lk1, L0_attn_a_lq2, L0_attn_a_lk2)
    x = x + _L0_ffn_ref(_layernorm(x, axis=-1), L0_ffn_router_w, L0_ffn_router_b, L0_ffn_sw1, L0_ffn_sb1, L0_ffn_sw2, L0_ffn_sb2, L0_ffn_rw1, L0_ffn_rb1, L0_ffn_rw2, L0_ffn_rb2)
    x = x + _L0_attn_b_ref(_layernorm(x, axis=-1), L0_attn_b_gamma_h, L0_attn_b_wq_h, L0_attn_b_wkv_h, L0_attn_b_wo_h, L0_attn_b_ln_g, L0_attn_b_ln_b, L0_attn_b_wqkv_l, L0_attn_b_wo_l, L0_attn_b_rt_q, L0_attn_b_rt_kv)
    x = x + _L0_ffn_ref(_layernorm(x, axis=-1), L0_ffn_router_w, L0_ffn_router_b, L0_ffn_sw1, L0_ffn_sb1, L0_ffn_sw2, L0_ffn_sb2, L0_ffn_rw1, L0_ffn_rb1, L0_ffn_rw2, L0_ffn_rb2)
    x = x + _L1_attn_a_ref(_layernorm(x, axis=-1), L1_attn_a_W_in, L1_attn_a_conv_w, L1_attn_a_conv_b, L1_attn_a_W_x, L1_attn_a_W_dt, L1_attn_a_b_dt, L1_attn_a_A_log, L1_attn_a_D, L1_attn_a_W_out)
    x = x + _L1_ffn_ref(_layernorm(x, axis=-1), L1_ffn_w_gate, L1_ffn_w_up, L1_ffn_w_down)
    x = x + _L1_attn_b_ref(_layernorm(x, axis=-1), L1_attn_b_Wq, L1_attn_b_bq, L1_attn_b_Wk, L1_attn_b_bk, L1_attn_b_Wv, L1_attn_b_bv, L1_attn_b_Wo, L1_attn_b_bo)
    x = x + _L1_ffn_ref(_layernorm(x, axis=-1), L1_ffn_w_gate, L1_ffn_w_up, L1_ffn_w_down)
    return x

_drawn_inputs = setup_inputs


def setup_inputs(seed=0):
    import zlib

    import numpy as np

    out = dict(_drawn_inputs(seed))
    spreads = {'L0_attn_b_gamma_h': (1.0, 0.6),
     'L0_attn_b_ln_g': (1.0, 0.6),
     'L0_attn_b_ln_b': (0.0, 0.406),
     'L0_ffn_router_b': (0.0, 0.1),
     'L0_ffn_sb1': (0.0, 0.1),
     'L0_ffn_sb2': (0.0, 0.1),
     'L0_ffn_rb1': (0.0, 0.475),
     'L0_ffn_rb2': (0.0, 0.1),
     'L1_attn_a_D': (1.0, 0.2),
     'L1_attn_b_bq': (0.0, 0.8),
     'L1_attn_b_bk': (0.0, 0.8),
     'L1_attn_b_bv': (0.0, 0.1),
     'L1_attn_b_bo': (0.0, 0.1)}
    factors = {'L0_attn_a_lq1': 7.371,
     'L0_attn_a_lq2': 5.508,
     'L0_attn_a_lk2': 3.478,
     'L0_attn_b_wq_h': 8.0,
     'L0_attn_b_rt_q': 3.901,
     'L0_attn_b_rt_kv': 5.619}
    for name, (base, spread) in spreads.items():
        noise = np.random.default_rng([zlib.crc32(name.encode()), seed]).standard_normal(out[name].shape)
        drawn = base * np.exp(spread * noise) if base else spread * noise
        out[name] = jnp.asarray(drawn.astype(out[name].dtype))
    for name, factor in factors.items():
        out[name] = (out[name] * factor).astype(out[name].dtype)
    return out
```

```python
import math
from contextlib import ExitStack

import numpy as np
import concourse.bass as bass
from concourse import mybir

F32 = mybir.dt.float32
BF16 = mybir.dt.bfloat16
U32 = mybir.dt.uint32
ALU = mybir.AluOpType
ACT = mybir.ActivationFunctionType
AX = mybir.AxisListType

P = 128
B, T, C = 8, 512, 256
NT = T // P
KC = C // P
BANK = 512
LN_EPS = 1e-5


def bcast(ap, axis, n):
    a = ap.unsqueeze(axis)
    shape = list(a.shape)
    shape[axis] = n
    return a.to_broadcast(shape)


class Semaphores:

    def __init__(self, nc):
        self.nc, self.all = nc, []

    def named(self, name):
        self.all.append(self.nc.alloc_semaphore(name))
        return self.all[-1]

    def __enter__(self):
        return self

    def __exit__(self, kind, *_):
        if kind is None:
            self.nc.clear_and_free_semaphores(self.all)
            self.nc.all_engine_barrier()


class Core:

    def __init__(self, nc, ctx):
        self.nc = nc
        self.res = ctx.enter_context(nc.sbuf_tensor("residual", [P, B, NT, C], F32))
        self.mv = ctx.enter_context(nc.sbuf_tensor("mean_var", [P, B, NT, 2], F32))
        self.rstd = ctx.enter_context(nc.sbuf_tensor("rstd", [P, B, NT], F32))
        self.std = ctx.enter_context(nc.sbuf_tensor("std", [P, B, NT], F32))
        self.mv1 = ctx.enter_context(nc.sbuf_tensor("mean_var_1", [P, NT, 2], F32))
        self.stats = ctx.enter_context(nc.sbuf_tensor("bn_stats", [P, NT, 6], F32))
        self.ident = ctx.enter_context(nc.sbuf_tensor("ident", [P, P], F32))
        self.xn = ctx.enter_context(nc.sbuf_tensor("x_normed", [P, NT, C], F32))
        self.xnT = ctx.enter_context(nc.sbuf_tensor("x_normed_T", [P, KC, T], F32))
        self.ps = ctx.enter_context(nc.psum_tensor("banks", [P, 8, BANK], F32))


def token_stats(core, dve, b):
    for t in range(NT):
        core.nc.vector.bn_stats(core.stats[:, t, :], core.res[:, b, t, :])
    dve.drain()
    for t in range(NT):
        core.nc.vector.bn_aggr(core.mv1[:, t, :], core.stats[:, t, :])
    dve.drain()
    core.nc.vector.tensor_copy(core.mv[:, b, :, :], core.mv1[:, :, :])


def add_to_residual(core, dve, b, product):
    core.nc.vector.tensor_tensor(core.res[:, b, :, :], product, core.res[:, b, :, :], ALU.add)
    dve.drain()
    token_stats(core, dve, b)


def std_of_tokens(core, act, std_ready):
    core.nc.scalar.activation(core.std[:, :, :], core.mv[:, :, :, 1], ACT.Sqrt, bias=core.eps[:, :],
                              scale=1.0).then_inc(std_ready, 1)


def rstd_of_tokens(core, dve, std_ready):
    dve.wait_ge(std_ready, 1)
    core.nc.vector.reciprocal(core.rstd[:, :, :], core.std[:, :, :])
    dve.drain()


def normalise(core, dve, b, xn_ready):
    for t in range(NT):
        last = core.nc.vector.tensor_scalar(core.xn[:, t, :], core.res[:, b, t, :], core.mv[:, b, t, 0:1],
                                            core.rstd[:, b, t:t + 1], ALU.subtract, ALU.mult)
    last.then_inc(xn_ready, 1)


def transpose_tokens(core, src, bank0):
    for c in range(KC):
        for t in range(NT):
            last = core.nc.tensor.transpose(core.ps[:, bank0 + c, t * P:(t + 1) * P],
                                            src[:, t, c * P:(c + 1) * P], core.ident[:, :])
    return last


DA_H = 8
DA_D = C // DA_H // 2
DA_LAMBDA = 0.8 - 0.6 * math.exp(-0.3 * 4)
RMS_EPS = float(np.finfo(np.float32).eps)


def diff_attention(core, w):
    nc, ps = core.nc, core.ps
    NH = 2 * DA_H
    HC = P // DA_D
    ctx = ExitStack()
    own = Semaphores(nc)
    with own, ctx:
        def sb(name, shape, dt=F32):
            return ctx.enter_context(nc.sbuf_tensor("da_" + name, shape, dt))

        def sem(name):
            return own.named("da_" + name)

        sq = sb("sq", [P, NT, 2 * C])
        ssum = sb("ssum", [P, NT, 2 * NH])
        sstd = sb("sstd", [P, NT, 2 * NH])
        srcp = sb("srcp", [P, NT, 2 * NH])
        qn = sb("qn", [P, 2 * C])
        rot = sb("rot", [P, 2 * C])
        qk = sq
        kT = sb("kT", [P, KC, T])
        qm = sb("qm", [P, NH, T])
        vx = sb("vx", [P, NT, DA_H, 64])
        pt = sb("pt", [P, 4, sum(T - j * P for j in range(NT))])
        at = [sum(T - i * P for i in range(j)) for j in range(NT)]
        osb = sb("osb", [P, 2, T])
        rr = sb("rr", [P, 2, NT, 2])
        t1 = sb("t1", [P, 2, NT, 32])
        tt2 = sb("t2", [P, 2, NT, 32])
        att = core.xn[:, :, :].rearrange("p t (h d) -> p t h d", d=32)
        mean = sb("mean", [P, NT * DA_H])
        outT = kT
        lam4 = sb("lam4", [P, 2, DA_D])
        lams = sb("lams", [P, 4])
        nlam = sb("nlam", [P, 1])
        lprod = sb("lprod", [P, 2, DA_D])

        s_std, s_ones, s_lam = sem("std"), sem("ones"), sem("lam")
        s_xn, s_xT, s_xnT = sem("xn"), sem("xT"), sem("xnT")
        s_qk, s_v, s_sq, s_ssum, s_sstd, s_rot = (sem(x) for x in ("qk", "v", "sq", "ssum", "sstd", "rot"))
        s_qkT, s_kT, s_qmA, s_qmD, s_vx = (sem(x) for x in ("qkT", "kT", "qmA", "qmD", "vx"))
        s_sc, s_exp, s_tri, s_av, s_osb, s_oT, s_att = (sem(x) for x in ("sc", "exp", "tri", "av", "osb", "oT", "att"))
        s_cen, s_sq2, s_var, s_std2, s_ln, s_attT, s_outT, s_y, s_res = (
            sem(x) for x in ("cen", "sq2", "var", "std2", "ln", "attT", "outT", "y", "res"))
        HV, SC = DA_H, NH * NT

        with nc.Block() as block:
            @block.tensor
            def _(pe):
                pe.wait_ge(core.loaded["da"], core.loads["da"])
                with pe.Fori(0, B) as b:
                    pe.wait_ge(s_xn, b + 1)
                    transpose_tokens(core, core.xn, 0).then_inc(s_xT, 1)
                    pe.wait_ge(s_xnT, b + 1)
                    for t in range(NT):
                        for c in range(KC):
                            last = nc.tensor.matmul(ps[:, 2 + t, :], core.xnT[:, c, t * P:(t + 1) * P],
                                                    w["da_wqk"][:, c, :], start=(c == 0), stop=(c == KC - 1))
                        last.then_inc(s_qk, 1)
                    for t in range(NT):
                        for c in range(KC):
                            last = nc.tensor.matmul(ps[:, 6 + t // 2, (t % 2) * C:(t % 2 + 1) * C],
                                                    core.xnT[:, c, t * P:(t + 1) * P],
                                                    w["da_wv"][:, c, :], start=(c == 0), stop=(c == KC - 1))
                    last.then_inc(s_v, 1)
                    pe.wait_ge(s_rot, b + 1)
                    for ch in range(2 * KC):
                        for t in range(NT):
                            last = nc.tensor.transpose(ps[:, 2 + ch, t * P:(t + 1) * P],
                                                       qk[:, t, ch * P:(ch + 1) * P], core.ident[:, :])
                        last.then_inc(s_qkT, 1)
                    pe.wait_ge(s_kT, b + 1)
                    pe.wait_ge(s_qmA, b + 1)
                    pe.wait_ge(s_qmD, b + 1)
                    pe.wait_ge(s_vx, b + 1)

                    def scores(hv):
                        for sub in range(2):
                            h = 2 * hv + sub
                            for j in range(NT):
                                n = h * NT + j
                                if n >= 4:
                                    pe.wait_ge(s_exp, b * SC + n - 3)
                                nc.tensor.matmul(ps[:, 2 + n % 4, 0:T - j * P],
                                                 kT[:, h // HC, j * P:(j + 1) * P], qm[:, h, j * P:T],
                                                 start=True, stop=True).then_inc(s_sc, 1)

                    def values(hv):
                        pe.wait_ge(s_tri, b * SC + (hv + 1) * 2 * NT)
                        if hv >= 2:
                            pe.wait_ge(s_osb, b * HV + hv - 1)
                        for j in range(NT):
                            for sub in range(2):
                                h = 2 * hv + sub
                                last = nc.tensor.matmul(ps[64 * sub:64 * sub + 64, 6 + hv % 2, j * P:T],
                                                        vx[:, j, hv, :], pt[:, h % 4, at[j]:at[j] + T - j * P],
                                                        start=(j == 0), stop=(j == NT - 1))
                        last.then_inc(s_av, 1)

                    def back(hv):
                        pe.wait_ge(s_osb, b * HV + hv + 1)
                        if hv >= 2:
                            pe.wait_ge(s_att, b * HV + hv - 1)
                        for t in range(NT):
                            last = nc.tensor.transpose(ps[:, hv % 2, t * P:(t + 1) * P],
                                                       osb[:, hv % 2, t * P:(t + 1) * P], core.ident[:, :])
                        last.then_inc(s_oT, 1)

                    scores(0)
                    for hv in range(HV):
                        if hv + 1 < HV:
                            scores(hv + 1)
                        values(hv)
                        if hv >= 1:
                            back(hv - 1)
                    back(HV - 1)
                    pe.wait_ge(s_ln, b + 1)
                    for c in range(KC):
                        for t in range(NT):
                            last = nc.tensor.transpose(ps[:, c, t * P:(t + 1) * P],
                                                       att[:, t, 4 * c:4 * c + 4, :], core.ident[:, :])
                    last.then_inc(s_attT, 1)
                    pe.wait_ge(s_outT, b + 1)
                    for t in range(NT):
                        for c in range(KC):
                            last = nc.tensor.matmul(ps[:, 6 + t // 2, (t % 2) * C:(t % 2 + 1) * C],
                                                    outT[:, c, t * P:(t + 1) * P],
                                                    w["da_wo"][:, c, :], start=(c == 0), stop=(c == KC - 1))
                    last.then_inc(s_y, 1)

            @block.scalar
            def _(act):
                std_of_tokens(core, act, s_std)
                act.wait_ge(s_lam, 1)
                nc.scalar.activation(lams[:, 2:4], lams[:, 0:2], ACT.Exp).then_inc(s_lam, 1)
                with act.Fori(0, B) as b:
                    act.wait_ge(s_xT, b + 1)
                    nc.scalar.copy(core.xnT[:, :, :], ps[:, 0:2, :]).then_inc(s_xnT, 1)
                    for t in range(NT):
                        act.wait_ge(s_qk, b * NT + t + 1)
                        nc.scalar.activation(sq[:, t, :], ps[:, 2 + t, :], ACT.Square).then_inc(s_sq, 1)
                    act.wait_ge(s_ssum, b + 1)
                    nc.scalar.activation(sstd[:, :, :], ssum[:, :, :], ACT.Sqrt, bias=core.rms_eps[:, :],
                                         scale=1.0 / DA_D).then_inc(s_sstd, 1)
                    act.wait_ge(s_qkT, b * 4 + 1)
                    for h in range(HC):
                        last = nc.scalar.mul(qm[:, h, :], ps[:, 2, :], w["da_hmask"][:, h:h + 1])
                    last.then_inc(s_qmA, 1)
                    act.wait_ge(s_qkT, b * 4 + 4)
                    nc.scalar.copy(kT[:, :, :], ps[:, 4:6, :]).then_inc(s_kT, 1)
                    for hv in range(HV + 1):
                        for sub in range(2):
                            h = 2 * hv + sub
                            for j in range(NT):
                                if hv == HV:
                                    break
                                n = h * NT + j
                                act.wait_ge(s_sc, b * SC + n + 1)
                                if h >= 4 and j == 0:
                                    act.wait_ge(s_av, b * HV + hv - 1)
                                nc.scalar.activation(pt[:, h % 4, at[j]:at[j] + T - j * P], ps[:, 2 + n % 4, 0:T - j * P],
                                                     ACT.Exp, scale=1.0 / math.sqrt(DA_D)).then_inc(s_exp, 1)
                        if hv >= 1:
                            act.wait_ge(s_av, b * HV + hv)
                            if hv >= 3:
                                act.wait_ge(s_oT, b * HV + hv - 2)
                            nc.scalar.copy(osb[:, (hv - 1) % 2, :], ps[:, 6 + (hv - 1) % 2, :]).then_inc(s_osb, 1)
                    act.wait_ge(s_cen, b + 1)
                    nc.scalar.activation(sq[:, :, 0:C], att[:, :, :, :].rearrange("p t h d -> p t (h d)"),
                                         ACT.Square).then_inc(s_sq2, 1)
                    act.wait_ge(s_var, b + 1)
                    nc.scalar.activation(sstd[:, :, 0:DA_H], ssum[:, :, 0:DA_H], ACT.Sqrt, bias=core.eps[:, :],
                                         scale=1.0 / 32).then_inc(s_std2, 1)
                    act.wait_ge(s_attT, b + 1)
                    nc.scalar.copy(outT[:, :, :], ps[:, 0:2, :]).then_inc(s_outT, 1)

            @block.vector
            def _(dve):
                nc.vector.memset(vx[:, :, :, 32:33], 1.0)
                nc.vector.memset(vx[:, :, :, 33:64], 0.0)
                nc.vector.tensor_tensor(lprod[:, :, :], w["da_lq"][:, :, :], w["da_lk"][:, :, :], ALU.mult)
                dve.drain()
                nc.vector.reduce_sum(lams[:, 0:2], lprod[:, :, :], axis=AX.X).then_inc(s_lam, 1)
                rstd_of_tokens(core, dve, s_std)
                dve.wait_ge(s_lam, 2)
                nc.vector.tensor_tensor(nlam[:, :], lams[:, 3:4], lams[:, 2:3], ALU.subtract)
                dve.drain()
                nc.vector.tensor_scalar(nlam[:, :], nlam[:, :], DA_LAMBDA, None, ALU.subtract)
                dve.drain()
                with dve.Fori(0, B) as b:
                    normalise(core, dve, b, s_xn)
                    for t in range(NT):
                        dve.wait_ge(s_sq, b * NT + t + 1)
                        nc.vector.reduce_sum(ssum[:, t, :], sq[:, t, :].rearrange("p (h d) -> p h d", d=DA_D),
                                             axis=AX.X)
                    dve.drain().then_inc(s_ssum, 1)
                    dve.wait_ge(s_sstd, b + 1)
                    nc.vector.reciprocal(srcp[:, :, :], sstd[:, :, :])
                    for t in range(NT):
                        dve.drain()
                        nc.vector.tensor_tensor(qn[:, :].rearrange("p (h d) -> p h d", d=DA_D),
                                                ps[:, 2 + t, :].rearrange("p (h d) -> p h d", d=DA_D),
                                                bcast(srcp[:, t, :], 2, DA_D), ALU.mult)
                        dve.drain()
                        nc.vector.tensor_tensor(rot[:, :].rearrange("p (h a d) -> p h a d", a=2, d=DA_D // 2),
                                                qn[:, :].rearrange("p (h a d) -> p h a d", a=2, d=DA_D // 2)[:, :, ::-1, :],
                                                bcast(w["da_sin"][:, t, :, :], 1, 2 * NH), ALU.mult)
                        nc.vector.tensor_tensor(qk[:, t, :].rearrange("p (h d) -> p h d", d=DA_D),
                                                qn[:, :].rearrange("p (h d) -> p h d", d=DA_D),
                                                bcast(w["da_cos"][:, t, :], 1, 2 * NH), ALU.mult)
                        dve.drain()
                        nc.vector.tensor_tensor(qk[:, t, :], qk[:, t, :], rot[:, :], ALU.add)
                    dve.drain().then_inc(s_rot, 1)
                    dve.wait_ge(s_v, b + 1)
                    for t2 in range(2):
                        last = nc.vector.tensor_copy(vx[:, 2 * t2:2 * t2 + 2, :, 0:32],
                                                     ps[:, 6 + t2, :].rearrange("p (t h d) -> p t h d", t=2, d=32))
                    last.then_inc(s_vx, 1)
                    dve.wait_ge(s_qkT, b * 4 + 2)
                    for h in range(HC):
                        last = nc.vector.tensor_scalar(qm[:, HC + h, :], ps[:, 3, :], w["da_hmask"][:, h:h + 1],
                                                       None, ALU.mult)
                    last.then_inc(s_qmD, 1)
                    for hv in range(HV):
                        r = hv % 2
                        dve.wait_ge(s_oT, b * HV + hv + 1)
                        sums = ps[:, r, :].rearrange("p (t s d) -> p t s d", t=NT, s=2)
                        nc.vector.reciprocal(rr[:, r, :, :], sums[:, :, :, 32])
                        dve.drain()
                        nc.vector.tensor_scalar(rr[:, r, :, 1:2], rr[:, r, :, 1:2], nlam[:, :], None, ALU.mult)
                        nc.vector.tensor_tensor(t1[:, r, :, :], sums[:, :, 0, 0:32], bcast(rr[:, r, :, 0], 2, 32), ALU.mult)
                        dve.drain()
                        nc.vector.tensor_tensor(tt2[:, r, :, :], sums[:, :, 1, 0:32], bcast(rr[:, r, :, 1], 2, 32), ALU.mult)
                        dve.drain()
                        nc.vector.tensor_tensor(att[:, :, hv, :], t1[:, r, :, :], tt2[:, r, :, :],
                                                ALU.add).then_inc(s_att, 1)
                    dve.drain()
                    heads = att[:, :, :, :].rearrange("p t h d -> p (t h) d")
                    nc.vector.reduce_sum(mean[:, :], heads, axis=AX.X)
                    dve.drain()
                    nc.vector.tensor_scalar(mean[:, :], mean[:, :], 1.0 / 32, None, ALU.mult)
                    dve.drain()
                    nc.vector.tensor_tensor(heads, heads, bcast(mean[:, :], 2, 32), ALU.subtract).then_inc(s_cen, 1)
                    dve.wait_ge(s_sq2, b + 1)
                    nc.vector.reduce_sum(ssum[:, :, 0:DA_H], sq[:, :, 0:C].rearrange("p t (h d) -> p t h d", d=32),
                                         axis=AX.X).then_inc(s_var, 1)
                    dve.wait_ge(s_std2, b + 1)
                    nc.vector.reciprocal(srcp[:, :, 0:DA_H], sstd[:, :, 0:DA_H])
                    dve.drain()
                    nc.vector.tensor_scalar(mean[:, :].rearrange("p (t h) -> p t h", t=NT), srcp[:, :, 0:DA_H],
                                            1.0 - DA_LAMBDA, None, ALU.mult)
                    dve.drain()
                    nc.vector.tensor_tensor(heads, heads, bcast(mean[:, :], 2, 32), ALU.mult).then_inc(s_ln, 1)
                    dve.wait_ge(s_y, b + 1)
                    add_to_residual(core, dve, b, ps[:, 6:8, :].rearrange("p a (t c) -> p (a t) c", t=2))
                    dve.drain()

            @block.gpsimd
            def _(pool):
                with pool.Fori(0, B) as b:
                    for h in range(NH):
                        for j in range(NT):
                            n = h * NT + j
                            pool.wait_ge(s_exp, b * SC + n + 1)
                            diag = pt[:, h % 4, at[j]:at[j] + P]
                            nc.gpsimd.tensor_tensor(diag, diag, w["da_tri"][:, :], ALU.mult).then_inc(s_tri, 1)


NE, TOPK = 8, 2
HID = 512
HCH = HID // P


def experts(core, w, a, tag):
    nc, ps = core.nc, core.ps
    NX = NE + 1
    ctx = ExitStack()
    own = Semaphores(nc)
    with own, ctx:
        def sb(name, shape, dt=F32):
            return ctx.enter_context(nc.sbuf_tensor(f"{tag}_" + name, shape, dt))

        def sem(name):
            return own.named(f"{tag}_" + name)

        lg = sb("logits", [P, NT, NE])
        mx = sb("mx", [P, NT])
        sm = sb("sm", [P, NT])
        rs = sb("rs", [P, NT])
        top = sb("top", [P, NT, 8])
        idx = sb("idx", [P, NT, 8], U32)
        idf = sb("idf", [P, NT, 8])
        wt = sb("wt", [P, NT, NX])
        wa = sb("wa", [P, NT, NE])
        wT = sb("wT", [NX, NT, P])
        hT = sb("hT", [P, 2, HCH, T])
        acc = sb("acc", [P, NT, C])

        w1 = sb("w1", [P, NX, KC, HID])
        w2 = sb("w2", [P, NX, HCH, C])
        s_w = [sem(f"w{e}") for e in range(NX)]
        s_std, s_xn, s_xT, s_xnT = sem("std"), sem("xn"), sem("xT"), sem("xnT")
        s_lg, s_lgs, s_exp, s_wt, s_wTp, s_wT, s_bias = (sem(x) for x in ("lg", "lgs", "exp", "wt", "wTp", "wT", "bias"))
        s_h, s_g, s_y, s_acc = sem("h"), sem("g"), sem("y"), sem("acc")

        with nc.Block() as block:
            @block.sync
            def _(sp):
                for e in range(NX):
                    sp.dma_start(w1[:, e, :, :], a["moe_w1"][e, :, :].rearrange("(c p) n -> p c n", p=P)).then_inc(s_w[e], 16)
                    sp.dma_start(w2[:, e, :, :], a["moe_w2"][e, :, :].rearrange("(m p) n -> p m n", p=P)).then_inc(s_w[e], 16)

            @block.tensor
            def _(pe):
                with pe.Fori(0, B) as b:
                    pe.wait_ge(s_xn, b + 1)
                    transpose_tokens(core, core.xn, 0).then_inc(s_xT, 1)
                    pe.wait_ge(s_xnT, b + 1)
                    for t in range(NT):
                        for c in range(KC):
                            last = nc.tensor.matmul(ps[:, 0, t * NE:(t + 1) * NE], core.xnT[:, c, t * P:(t + 1) * P],
                                                    w["moe_router"][:, c, :], start=(c == 0), stop=(c == KC - 1))
                    last.then_inc(s_lg, 1)

                    def up(e):
                        pe.wait_ge(s_w[e], 32)
                        for m in range(HCH):
                            n = e * HCH + m
                            if n >= 4:
                                pe.wait_ge(s_g, b * NX * HCH + n - 3)
                            for c in range(KC):
                                last = nc.tensor.matmul(ps[:, 2 + n % 4, :], w1[:, e, c, m * P:(m + 1) * P],
                                                        core.xnT[:, c, :], start=(c == 0), stop=(c == KC - 1))
                            last.then_inc(s_h, 1)

                    def down(e):
                        pe.wait_ge(s_g, b * NX * HCH + (e + 1) * HCH)
                        for t in range(NT):
                            n = e * 2 + t // 2
                            if n >= 2 and t % 2 == 0:
                                pe.wait_ge(s_acc, b * NX * 2 + n - 1)
                            for m in range(HCH):
                                last = nc.tensor.matmul(ps[:, 6 + t // 2, (t % 2) * C:(t % 2 + 1) * C],
                                                        hT[:, e % 2, m, t * P:(t + 1) * P], w2[:, e, m, :],
                                                        start=(m == 0), stop=(m == HCH - 1))
                            if t % 2:
                                last.then_inc(s_y, 1)

                    up(0)
                    pe.wait_ge(s_wt, b + 1)
                    for t in range(NT):
                        last = nc.tensor.transpose(ps[0:NX, 1, t * P:(t + 1) * P], wt[:, t, :], core.ident[:, :])
                    last.then_inc(s_wTp, 1)
                    pe.wait_ge(s_wT, b + 1)
                    for t in range(NT):
                        last = nc.tensor.matmul(ps[:, t // 2, (t % 2) * C:(t % 2 + 1) * C], wT[:, t, :],
                                                w["moe_b2"][:, :], start=True, stop=True)
                    last.then_inc(s_bias, 1)
                    for e in range(NX):
                        if e + 1 < NX:
                            up(e + 1)
                        down(e)

            @block.scalar
            def _(act):
                std_of_tokens(core, act, s_std)
                with act.Fori(0, B) as b:
                    act.wait_ge(s_xT, b + 1)
                    nc.scalar.copy(core.xnT[:, :, :], ps[:, 0:2, :]).then_inc(s_xnT, 1)
                    act.wait_ge(s_lgs, b + 1)
                    nc.scalar.activation(lg[:, :, :], lg[:, :, :], ACT.Exp).then_inc(s_exp, 1)
                    act.wait_ge(s_wTp, b + 1)
                    nc.scalar.copy(wT[:, :, :], ps[0:NX, 1, :].rearrange("p (t q) -> p t q", t=NT)).then_inc(s_wT, 1)
                    for e in range(NX):
                        if e >= 2:
                            act.wait_ge(s_y, b * NX * 2 + (e - 1) * 2)
                        for m in range(HCH):
                            n = e * HCH + m
                            act.wait_ge(s_h, b * NX * HCH + n + 1)
                            nc.scalar.activation(hT[:, e % 2, m, :], ps[:, 2 + n % 4, :], ACT.Gelu,
                                                 bias=w["moe_b1"][:, e, m:m + 1]).then_inc(s_g, 1)

            @block.vector
            def _(dve):
                nc.vector.memset(wt[:, :, NE:NX], 1.0)
                rstd_of_tokens(core, dve, s_std)
                with dve.Fori(0, B) as b:
                    normalise(core, dve, b, s_xn)
                    dve.wait_ge(s_lg, b + 1)
                    nc.vector.tensor_tensor(lg[:, :, :], ps[:, 0, 0:NT * NE].rearrange("p (t e) -> p t e", e=NE),
                                            bcast(w["moe_rb"][:, :], 1, NT), ALU.add)
                    dve.drain()
                    nc.vector.reduce_max(mx[:, :], lg[:, :, :], axis=AX.X)
                    dve.drain()
                    nc.vector.tensor_tensor(lg[:, :, :], lg[:, :, :], bcast(mx[:, :], 2, NE),
                                            ALU.subtract).then_inc(s_lgs, 1)
                    dve.wait_ge(s_exp, b + 1)
                    nc.vector.reduce_sum(sm[:, :], lg[:, :, :], axis=AX.X)
                    dve.drain()
                    nc.vector.reciprocal(rs[:, :], sm[:, :])
                    dve.drain()
                    nc.vector.tensor_tensor(lg[:, :, :], lg[:, :, :], bcast(rs[:, :], 2, NE), ALU.mult)
                    dve.drain()
                    for t in range(NT):
                        nc.vector.max(top[:, t, :], lg[:, t, :])
                    dve.drain()
                    for t in range(NT):
                        nc.vector.max_index(idx[:, t, :], top[:, t, :], lg[:, t, :])
                    dve.drain()
                    nc.vector.tensor_copy(idf[:, :, :], idx[:, :, :])
                    dve.drain()
                    for t in range(NT):
                        nc.vector.tensor_scalar(wa[:, t, :], w["moe_iota"][:, :], idf[:, t, 0:1], top[:, t, 0:1],
                                                ALU.is_equal, ALU.mult)
                        nc.vector.tensor_scalar(wt[:, t, 0:NE], w["moe_iota"][:, :], idf[:, t, 1:2], top[:, t, 1:2],
                                                ALU.is_equal, ALU.mult)
                    dve.drain()
                    nc.vector.tensor_tensor(wt[:, :, 0:NE], wt[:, :, 0:NE], wa[:, :, :], ALU.add)
                    dve.drain().then_inc(s_wt, 1)
                    dve.wait_ge(s_bias, b + 1)
                    nc.vector.tensor_tensor(acc[:, :, :], ps[:, 0:2, :].rearrange("p a (t c) -> p (a t) c", t=2),
                                            core.res[:, b, :, :], ALU.add)
                    for e in range(NX):
                        dve.drain()
                        for t in range(NT):
                            if t % 2 == 0:
                                dve.wait_ge(s_y, b * NX * 2 + e * 2 + t // 2 + 1)
                            last = nc.vector.scalar_tensor_tensor(
                                acc[:, t, :], ps[:, 6 + t // 2, (t % 2) * C:(t % 2 + 1) * C],
                                wt[:, t, e:e + 1], acc[:, t, :], ALU.mult, ALU.add)
                            if t % 2:
                                last.then_inc(s_acc, 1)
                    dve.drain()
                    nc.vector.tensor_copy(core.res[:, b, :, :], acc[:, :, :])
                    dve.drain()
                    token_stats(core, dve, b)
                    dve.drain()


LB_H, LB_D, LB_W = 8, 64, 64
LB_SEL = 256
LB_I = LB_H * LB_D
LB_FC = LB_I // P
LB_ST = LB_SEL // P


def routed_attention(core, w):
    nc, ps = core.nc, core.ps
    items = [("light", qt, h, max(0, qt - 1), min(NT - 1, qt + 1)) for qt in range(NT) for h in range(LB_H)]
    items += [("heavy", qt, h, 0, LB_ST - 1) for qt in range(LB_ST) for h in range(LB_H)]
    NI, NG = len(items), len(items) // LB_H
    ctx = ExitStack()
    own = Semaphores(nc)
    with own, ctx:
        def sb(name, shape, dt=F32):
            return ctx.enter_context(nc.sbuf_tensor("lb_" + name, shape, dt))

        def sem(name):
            return own.named("lb_" + name)

        st2 = sb("st2", [P, NT, 6])
        mv2 = sb("mv2", [P, NT, 2])
        sd2 = sb("sd2", [P, 2 * NT])
        rc2 = sb("rc2", [P, 2 * NT])
        ssq = sb("ssq", [P, NT])
        xl = sb("xl", [P, NT, C])
        xlT = sb("xlT", [P, KC, T])
        hn = sb("hn", [P, NT, C])
        junk = sb("junk", [P, C])
        qm = sb("qm", [P, LB_H, T])
        kT = sb("kT", [P, LB_FC, T])
        v = sb("v", [P, NT, LB_I])
        rep = sb("rep", [P, 2, KC, P])
        sbc = sb("sbc", [P, 2, T])
        scol = sb("scol", [P, 2, NT])
        cmp = sb("cmp", [P, NT, T], BF16)
        eq = sb("eq", [P, P])
        tj = sb("tj", [P, P])
        onb = sb("onb", [P, P], BF16)
        identb = sb("identb", [P, P], BF16)
        maskb = sb("maskb", [P, 3 * P], BF16)
        rkb = sb("rkb", [P, T])
        rkc = sb("rkc", [P, NT])
        oh = sb("oh", [P, NT, LB_SEL])
        back = sb("back", [P, LB_ST, T])
        gT = sb("gT", [P, 2, KC, LB_SEL])
        hqm = sb("hqm", [P, LB_H, LB_SEL])
        hkT = sb("hkT", [P, LB_FC, LB_SEL])
        hv = sb("hv", [P, LB_ST, LB_I])
        nmx = sb("nmx", [P, 4])
        sums = sb("sums", [P, 2, LB_H])
        rs = sb("rs", [P, 2, LB_H])
        pq = sb("pq", [P, 4, 3 * P])
        pt = sb("pt", [P, 4, 3 * P])
        lo = sb("lo", [P, 2, LB_I])
        loT = sb("loT", [P, NG, LB_FC, P])
        hh = sb("hh", [P, LB_ST, C])

        s_std, s_b, s_rep, s_xn, s_ss, s_vr, s_sd, s_xl, s_hn, s_xT, s_xnT, s_xlT = (
            sem(x) for x in ("std", "b", "rep", "xn", "ss", "vr", "sd", "xl", "hn", "xT", "xnT", "xlT"))
        s_sc, s_cmp, s_rk, s_oh, s_g, s_gT, s_back = (sem(x) for x in ("sc", "cmp", "rk", "oh", "g", "gT", "back"))
        s_q, s_qm, s_k, s_kT, s_v, s_vc, s_hq, s_hqm, s_hk, s_hkT, s_hv, s_hvc = (
            sem(x) for x in ("q", "qm", "k", "kT", "v", "vc", "hq", "hqm", "hk", "hkT", "hv", "hvc"))
        s_s, s_mx, s_e, s_tp, s_t, s_av, s_lo, s_loTp, s_loT, s_hh, s_hhc, s_y = (
            sem(x) for x in ("s", "mx", "e", "tp", "t", "av", "lo", "loTp", "loT", "hh", "hhc", "y"))

        with nc.Block() as block:
            @block.tensor
            def _(pe):
                pe.wait_ge(core.loaded["lb"], core.loads["lb"])
                pe.wait_ge(s_rep, 1)
                with pe.Fori(0, B) as b:
                    pe.wait_ge(s_xn, b + 1)
                    transpose_tokens(core, core.xn, 0).then_inc(s_xT, 1)
                    pe.wait_ge(s_xl, b + 1)
                    transpose_tokens(core, xl, 2).then_inc(s_xT, 1)
                    pe.wait_ge(s_xnT, b + 1)
                    for r in range(2):
                        for c in range(KC):
                            last = nc.tensor.matmul(ps[:, 4 + r, :], rep[:, r, c, :], core.xnT[:, c, :],
                                                    start=(c == 0), stop=(c == KC - 1))
                        last.then_inc(s_sc, 1)
                    pe.wait_ge(s_xlT, b + 1)
                    for m in range(LB_FC):
                        if m >= 2:
                            pe.wait_ge(s_qm, b * LB_FC + m - 1)
                        for c in range(KC):
                            last = nc.tensor.matmul(ps[:, m % 2, :], w["lb_wqkv"][:, c, m * P:(m + 1) * P],
                                                    xlT[:, c, :], start=(c == 0), stop=(c == KC - 1))
                        last.then_inc(s_q, 1)
                    for m in range(LB_FC):
                        if m >= 2:
                            pe.wait_ge(s_kT, b * LB_FC + m - 1)
                        for c in range(KC):
                            last = nc.tensor.matmul(ps[:, 2 + m % 2, :], w["lb_wqkv"][:, c, LB_I + m * P:LB_I + (m + 1) * P],
                                                    xlT[:, c, :], start=(c == 0), stop=(c == KC - 1))
                        last.then_inc(s_k, 1)
                    for t in range(NT):
                        if t < 2:
                            pe.wait_ge(s_qm, b * LB_FC + 3 + t)
                        else:
                            pe.wait_ge(s_vc, b * NT + t - 1)
                        for c in range(KC):
                            last = nc.tensor.matmul(ps[:, t % 2, :], xlT[:, c, t * P:(t + 1) * P],
                                                    w["lb_wqkv"][:, c, 2 * LB_I:3 * LB_I],
                                                    start=(c == 0), stop=(c == KC - 1))
                        last.then_inc(s_v, 1)
                    pe.wait_ge(s_hn, b + 1)
                    for r in range(2):
                        pe.wait_ge(s_cmp, 2 * b + r + 1)
                        for t in range(NT):
                            last = nc.tensor.matmul(ps[:, 6, :], onb[:, :], cmp[:, t, :],
                                                    start=(t == 0), stop=(t == NT - 1))
                        last.then_inc(s_rk, 1)
                        pe.wait_ge(s_oh, 2 * b + r + 1)
                        for c in range(KC):
                            for t in range(NT):
                                last = nc.tensor.matmul(ps[:, 7, c * LB_SEL:(c + 1) * LB_SEL],
                                                        hn[:, t, c * P:(c + 1) * P], oh[:, t, :],
                                                        start=(t == 0), stop=(t == NT - 1))
                        last.then_inc(s_g, 1)
                        pe.wait_ge(s_gT, 2 * b + r + 1)
                    for m in range(LB_FC):
                        for c in range(KC):
                            last = nc.tensor.matmul(ps[:, 4 + m // 2, (m % 2) * LB_SEL:(m % 2 + 1) * LB_SEL],
                                                    w["lb_wqh"][:, c, m * P:(m + 1) * P], gT[:, 0, c, :],
                                                    start=(c == 0), stop=(c == KC - 1))
                    last.then_inc(s_hq, 1)
                    for m in range(LB_FC):
                        for c in range(KC):
                            last = nc.tensor.matmul(ps[:, 6 + m // 2, (m % 2) * LB_SEL:(m % 2 + 1) * LB_SEL],
                                                    w["lb_wkvh"][:, c, m * P:(m + 1) * P], gT[:, 1, c, :],
                                                    start=(c == 0), stop=(c == KC - 1))
                    last.then_inc(s_hk, 1)
                    pe.wait_ge(s_kT, b * LB_FC + LB_FC)
                    for t in range(LB_ST):
                        for c in range(KC):
                            last = nc.tensor.matmul(ps[:, 2 + t, :], gT[:, 1, c, t * P:(t + 1) * P],
                                                    w["lb_wkvh"][:, c, LB_I:2 * LB_I],
                                                    start=(c == 0), stop=(c == KC - 1))
                    last.then_inc(s_hv, 1)
                    pe.wait_ge(s_hqm, b + 1)
                    pe.wait_ge(s_hkT, b + 1)
                    pe.wait_ge(s_hvc, b + 1)
                    pe.wait_ge(s_vc, b * NT + NT)

                    def scores(n):
                        kind, qt, h, j0, j1 = items[n]
                        if n >= 3:
                            pe.wait_ge(s_e, b * NI + n - 2)
                        width = (j1 - j0 + 1) * P
                        bank = ps[:, n % 3, 0:width]
                        if kind == "light":
                            off = (j0 - qt + 1) * P
                            nc.tensor.matmul(bank, qm[:, h, qt * P:(qt + 1) * P], kT[:, h // 2, j0 * P:(j1 + 1) * P],
                                             start=True, stop=False)
                            last = nc.tensor.matmul(bank, identb[:, :], maskb[:, off:off + width], start=False, stop=True)
                        else:
                            last = nc.tensor.matmul(bank, hqm[:, h, qt * P:(qt + 1) * P], hkT[:, h // 2, :],
                                                    start=True, stop=True)
                        last.then_inc(s_s, 1)

                    def turn(n):
                        kind, qt, h, j0, j1 = items[n]
                        pe.wait_ge(s_e, b * NI + n + 1)
                        if n >= 2:
                            pe.wait_ge(s_t, b * NI + n - 1)
                        for j in range(j1 - j0 + 1):
                            last = nc.tensor.transpose(ps[:, 3 + n % 2, j * P:(j + 1) * P],
                                                       pq[:, n % 4, j * P:(j + 1) * P], core.ident[:, :])
                        last.then_inc(s_tp, 1)

                    def values(n):
                        kind, qt, h, j0, j1 = items[n]
                        g = n // LB_H
                        pe.wait_ge(s_t, b * NI + n + 1)
                        if h == 0 and g >= 2:
                            pe.wait_ge(s_lo, b * NG + g - 1)
                        for j in range(j0, j1 + 1):
                            src = v if kind == "light" else hv
                            last = nc.tensor.matmul(ps[:, 5 + g % 2, h * LB_D:(h + 1) * LB_D],
                                                    pt[:, n % 4, (j - j0) * P:(j - j0 + 1) * P],
                                                    src[:, j, h * LB_D:(h + 1) * LB_D],
                                                    start=(j == j0), stop=(j == j1))
                        last.then_inc(s_av, 1)

                    def heads(g):
                        pe.wait_ge(s_lo, b * NG + g + 1)
                        if g >= 1:
                            pe.wait_ge(s_loT, b * NG + g)
                        for m in range(LB_FC):
                            last = nc.tensor.transpose(ps[:, 7, m * P:(m + 1) * P], lo[:, g % 2, m * P:(m + 1) * P],
                                                       core.ident[:, :])
                        last.then_inc(s_loTp, 1)

                    for n in range(2):
                        scores(n)
                    for n in range(NI + 8):
                        if n + 2 < NI:
                            scores(n + 2)
                        if n < NI:
                            turn(n)
                        if 0 <= n - 2 < NI:
                            values(n - 2)
                        if n >= 13 and (n - 13) % 8 == 0:
                            heads((n - 13) // 8)
                    assert (NI + 7 - 13) // 8 == NG - 1
                    pe.wait_ge(s_loT, b * NG + NG)
                    for t in range(LB_ST):
                        for m in range(LB_FC):
                            last = nc.tensor.matmul(ps[:, 0, t * C:(t + 1) * C], loT[:, NT + t, m, :],
                                                    w["lb_woh"][:, m, :], start=(m == 0), stop=(m == LB_FC - 1))
                    last.then_inc(s_hh, 1)
                    pe.wait_ge(s_hhc, b + 1)
                    for t in range(NT):
                        bank = ps[:, 1 + t // 2, (t % 2) * C:(t % 2 + 1) * C]
                        for m in range(LB_FC):
                            nc.tensor.matmul(bank, loT[:, t, m, :], w["lb_wol"][:, m, :], start=(m == 0), stop=False)
                        for r in range(LB_ST):
                            last = nc.tensor.matmul(bank, back[:, r, t * P:(t + 1) * P], hh[:, r, :],
                                                    start=False, stop=(r == LB_ST - 1))
                    last.then_inc(s_y, 1)

            @block.scalar
            def _(act):
                std_of_tokens(core, act, s_std)
                with act.Fori(0, B) as b:
                    act.wait_ge(s_xn, b + 1)
                    for t in range(NT):
                        nc.scalar.activation(junk[:, :], core.xn[:, t, :], ACT.Square, accum_out=ssq[:, t:t + 1])
                        act.drain()
                    act.wait_ge(s_vr, b + 1)
                    nc.scalar.activation(sd2[:, 0:NT], mv2[:, :, 1], ACT.Sqrt, bias=core.eps[:, :], scale=1.0)
                    nc.scalar.activation(sd2[:, NT:2 * NT], ssq[:, :], ACT.Sqrt)
                    act.drain().then_inc(s_sd, 1)
                    act.wait_ge(s_xT, 2 * b + 1)
                    nc.scalar.copy(core.xnT[:, :, :], ps[:, 0:2, :]).then_inc(s_xnT, 1)
                    act.wait_ge(s_xT, 2 * b + 2)
                    for c in range(KC):
                        last = nc.scalar.activation(xlT[:, c, :], ps[:, 2 + c, :], ACT.Identity,
                                                    bias=w["lb_lnb"][:, c:c + 1], scale=w["lb_lng"][:, c:c + 1])
                    last.then_inc(s_xlT, 1)
                    for m in range(LB_FC):
                        act.wait_ge(s_q, b * LB_FC + m + 1)
                        for i in range(2):
                            last = nc.scalar.mul(qm[:, 2 * m + i, :], ps[:, m % 2, :], w["lb_hmask"][:, i:i + 1])
                        last.then_inc(s_qm, 1)
                    for m in range(LB_FC):
                        act.wait_ge(s_k, b * LB_FC + m + 1)
                        nc.scalar.copy(kT[:, m, :], ps[:, 2 + m % 2, :]).then_inc(s_kT, 1)
                    for t in range(NT):
                        act.wait_ge(s_v, b * NT + t + 1)
                        nc.scalar.copy(v[:, t, :], ps[:, t % 2, :]).then_inc(s_vc, 1)
                    for r in range(2):
                        act.wait_ge(s_g, 2 * b + r + 1)
                        for c in range(KC):
                            last = nc.scalar.mul(gT[:, r, c, :], ps[:, 7, c * LB_SEL:(c + 1) * LB_SEL],
                                                 w["lb_gamma"][:, c:c + 1])
                        last.then_inc(s_gT, 1)
                    act.wait_ge(s_hq, b + 1)
                    for i in range(2):
                        last = nc.scalar.mul(hqm[:, i::2, :], ps[:, 4:6, :].rearrange("p a (m q) -> p (a m) q", m=2),
                                             w["lb_hmask"][:, i:i + 1])
                    last.then_inc(s_hqm, 1)
                    act.wait_ge(s_hv, b + 1)
                    nc.scalar.copy(hv[:, :, :], ps[:, 2:4, :]).then_inc(s_hvc, 1)
                    for n in range(NI + 8):
                        if n < NI:
                            kind, qt, h, j0, j1 = items[n]
                            width, g = (j1 - j0 + 1) * P, n // LB_H
                            act.wait_ge(s_mx, b * NI + n + 1)
                            if n >= 4:
                                act.wait_ge(s_tp, b * NI + n - 3)
                            if h == 0 and g >= 2:
                                act.wait_ge(s_lo, b * NG + g - 1)
                            nc.scalar.activation(pq[:, n % 4, 0:width], ps[:, n % 3, 0:width], ACT.Exp,
                                                 bias=nmx[:, n % 4:n % 4 + 1], accum_out=sums[:, g % 2, h:h + 1])
                            act.drain().then_inc(s_e, 1)
                        if n >= 15 and (n - 15) % 8 == 0:
                            g = (n - 15) // 8
                            act.wait_ge(s_loTp, b * NG + g + 1)
                            nc.scalar.copy(loT[:, g, :, :], ps[:, 7, :].rearrange("p (m q) -> p m q", m=LB_FC)).then_inc(s_loT, 1)
                    assert (NI + 7 - 15) // 8 == NG - 1
                    act.wait_ge(s_hh, b + 1)
                    nc.scalar.copy(hh[:, :, :], ps[:, 0, :].rearrange("p (t c) -> p t c", t=LB_ST)).then_inc(s_hhc, 1)

            @block.vector
            def _(dve):
                dve.wait_ge(core.loaded["lb"], core.loads["lb"])
                nc.vector.memset(onb[:, :], 1.0)
                nc.vector.tensor_copy(identb[:, :], core.ident[:, :])
                nc.vector.tensor_copy(maskb[:, :], w["lb_mask"][:, :])
                for r in range(2):
                    for c in range(KC):
                        nc.vector.tensor_copy(rep[:, r, c, :], w["lb_rt"][:, r, c:c + 1].to_broadcast([P, P]))
                dve.drain().then_inc(s_rep, 1)
                rstd_of_tokens(core, dve, s_std)
                with dve.Fori(0, B) as b:
                    normalise(core, dve, b, s_xn)
                    dve.drain()
                    for t in range(NT):
                        nc.vector.bn_stats(st2[:, t, :], core.xn[:, t, :])
                    dve.drain()
                    for t in range(NT):
                        nc.vector.bn_aggr(mv2[:, t, :], st2[:, t, :])
                    dve.drain().then_inc(s_vr, 1)
                    dve.wait_ge(s_sd, b + 1)
                    nc.vector.tensor_scalar(sd2[:, NT:2 * NT], sd2[:, NT:2 * NT], 1e-12, None, ALU.max)
                    dve.drain()
                    nc.vector.reciprocal(rc2[:, :], sd2[:, :])
                    dve.drain()
                    for t in range(NT):
                        last = nc.vector.tensor_scalar(xl[:, t, :], core.xn[:, t, :], mv2[:, t, 0:1], rc2[:, t:t + 1],
                                                       ALU.subtract, ALU.mult)
                    last.then_inc(s_xl, 1)
                    for t in range(NT):
                        last = nc.vector.tensor_scalar(hn[:, t, :], core.xn[:, t, :], rc2[:, NT + t:NT + t + 1],
                                                       float(C) ** 0.5, ALU.mult, ALU.mult)
                    last.then_inc(s_hn, 1)
                    for r in range(2):
                        dve.wait_ge(s_sc, 2 * b + r + 1)
                        nc.vector.tensor_copy(sbc[:, r, :], ps[:, 4 + r, :])
                        dve.drain()
                        for t in range(NT):
                            nc.vector.tensor_tensor_reduce(out=tj[:, :], in0=sbc[:, r, t * P:(t + 1) * P],
                                                           in1=core.ident[:, :], scale=1.0, scalar=0.0,
                                                           op0=ALU.mult, op1=ALU.add,
                                                           accum_out=scol[:, r, t:t + 1])
                            dve.drain()
                        for t in range(NT):
                            s = scol[:, r, t:t + 1]
                            lo_c, hi_c = t * P, (t + 1) * P
                            if lo_c:
                                nc.vector.tensor_scalar(cmp[:, t, 0:lo_c], sbc[:, r, 0:lo_c], s, None, ALU.is_le)
                            if hi_c < T:
                                nc.vector.tensor_scalar(cmp[:, t, hi_c:T], sbc[:, r, hi_c:T], s, None, ALU.is_lt)
                            dve.drain()
                            nc.vector.scalar_tensor_tensor(eq[:, :], sbc[:, r, lo_c:hi_c], s, w["lb_later"][:, :],
                                                           ALU.is_equal, ALU.mult)
                            dve.drain()
                            nc.vector.scalar_tensor_tensor(cmp[:, t, lo_c:hi_c], sbc[:, r, lo_c:hi_c], s, eq[:, :],
                                                           ALU.is_lt, ALU.add)
                        dve.drain().then_inc(s_cmp, 1)
                        dve.wait_ge(s_rk, 2 * b + r + 1)
                        nc.vector.tensor_copy(rkb[:, :], ps[:, 6, :])
                        dve.drain()
                        for t in range(NT):
                            nc.vector.tensor_tensor_reduce(out=tj[:, :], in0=rkb[:, t * P:(t + 1) * P],
                                                           in1=core.ident[:, :], scale=1.0, scalar=0.0,
                                                           op0=ALU.mult, op1=ALU.add, accum_out=rkc[:, t:t + 1])
                            dve.drain()
                        for t in range(NT):
                            nc.vector.tensor_scalar(oh[:, t, :], w["lb_iota"][:, :], rkc[:, t:t + 1], None, ALU.is_equal)
                        dve.drain().then_inc(s_oh, 1)
                        if r == 0:
                            for k in range(LB_ST):
                                nc.vector.tensor_scalar(back[:, k, :], rkb[:, :], w["lb_place"][:, k:k + 1], None,
                                                        ALU.is_equal)
                            dve.drain()
                        dve.wait_ge(s_g, 2 * b + r + 1)
                    dve.wait_ge(s_hk, b + 1)
                    nc.vector.tensor_copy(hkT[:, :, :], ps[:, 6:8, :].rearrange("p a (m q) -> p (a m) q", m=2)).then_inc(s_hkT, 1)
                    for n in range(NI + 8):
                        if n < NI:
                            kind, qt, h, j0, j1 = items[n]
                            width = (j1 - j0 + 1) * P
                            dve.wait_ge(s_s, b * NI + n + 1)
                            if n >= 4:
                                dve.wait_ge(s_e, b * NI + n - 3)
                            nc.vector.tensor_reduce(nmx[:, n % 4:n % 4 + 1], ps[:, n % 3, 0:width], op=ALU.max,
                                                    axis=AX.X, negate=True).then_inc(s_mx, 1)
                        m = n - 2
                        if 0 <= m < NI:
                            kind, qt, h, j0, j1 = items[m]
                            width = (j1 - j0 + 1) * P
                            dve.wait_ge(s_tp, b * NI + m + 1)
                            if m >= 4:
                                dve.wait_ge(s_av, b * NI + m - 3)
                            nc.vector.tensor_copy(pt[:, m % 4, 0:width], ps[:, 3 + m % 2, 0:width]).then_inc(s_t, 1)
                        if n >= 12 and (n - 12) % 8 == 0:
                            g = (n - 12) // 8
                            dve.wait_ge(s_av, b * NI + (g + 1) * LB_H)
                            if g >= 2:
                                dve.wait_ge(s_loTp, b * NG + g - 1)
                            nc.vector.reciprocal(rs[:, g % 2, :], sums[:, g % 2, :])
                            dve.drain()
                            nc.vector.tensor_tensor(lo[:, g % 2, :].rearrange("p (h d) -> p h d", d=LB_D),
                                                    ps[:, 5 + g % 2, :].rearrange("p (h d) -> p h d", d=LB_D),
                                                    bcast(rs[:, g % 2, :], 2, LB_D), ALU.mult).then_inc(s_lo, 1)
                    assert (NI + 7 - 12) // 8 == NG - 1
                    dve.wait_ge(s_y, b + 1)
                    add_to_residual(core, dve, b, ps[:, 1:3, :].rearrange("p a (t c) -> p (a t) c", t=2))
                    dve.drain()


MB_E, MB_N, MB_TAPS = 2 * C, 16, 4
MB_EC = MB_E // P
MB_LV = 7


def state_space(core, w):
    nc, ps = core.nc, core.ps
    ctx = ExitStack()
    own = Semaphores(nc)
    with own, ctx:
        def sb(name, shape, dt=F32):
            return ctx.enter_context(nc.sbuf_tensor("mb_" + name, shape, dt))

        def sem(name):
            return own.named("mb_" + name)

        HALO = MB_TAPS - 1
        xi = sb("xi", [P, MB_EC, HALO + T])
        cv = sb("cv", [P, MB_EC, T])
        uT = sb("uT", [P, MB_EC, T])
        ut = sb("ut", [P, NT, MB_E])
        gz = sb("gz", [P, NT, MB_E])
        yT = cv
        ax = sb("ax", [P, T])
        rl = sb("rl", [P, T])
        ex = sb("ex", [P, T])
        lp = sb("lp", [P, T])
        delta = sb("delta", [P, T])
        dA = sb("dA", [P, T + 2])
        dB = sb("dB", [P, T])
        fw = sb("fw", [P, T])
        bw = sb("bw", [P, T])
        cf = sb("cf", [P, T])
        bs = sb("bs", [P, T])
        cdp = sb("cdp", [P, T])
        cd = sb("cd", [P, NT])
        cfm = sb("cfm", [P, 8, T])
        bst = sb("bst", [P, NT, P])
        mm = sb("mm", [P, MB_LV, P])
        ms = sb("ms", [P, 2, P])
        hs = sb("hs", [P, 2, MB_E])
        v1 = sb("v1", [P, 2, MB_E])
        na = sb("na", [P, 1])

        s_std, s_A, s_xn, s_xT, s_xnT, s_xi, s_xic, s_z, s_gz, s_cv, s_u = (
            sem(x) for x in ("std", "A", "xn", "xT", "xnT", "xi", "xic", "z", "gz", "cv", "u"))
        s_utp, s_ut, s_dbc, s_pos, s_ln, s_delta, s_dA, s_cf, s_cd, s_bstp, s_bst = (
            sem(x) for x in ("utp", "ut", "dbc", "pos", "ln", "delta", "dA", "cf", "cd", "bstp", "bst"))
        s_p, s_m, s_hp, s_h, s_yp, s_y, s_yTp, s_yT, s_o = (
            sem(x) for x in ("p", "m", "hp", "h", "yp", "y", "yTp", "yT", "o"))

        with nc.Block() as block:
            @block.tensor
            def _(pe):
                pe.wait_ge(core.loaded["mb"], core.loads["mb"])
                with pe.Fori(0, B) as b:
                    pe.wait_ge(s_xn, b + 1)
                    transpose_tokens(core, core.xn, 0).then_inc(s_xT, 1)
                    pe.wait_ge(s_xnT, b + 1)
                    for m in range(MB_EC):
                        for c in range(KC):
                            last = nc.tensor.matmul(ps[:, 2 + m, :], w["mb_win"][:, c, m * P:(m + 1) * P],
                                                    core.xnT[:, c, :], start=(c == 0), stop=(c == KC - 1))
                        last.then_inc(s_xi, 1)
                    for t in range(NT):
                        if t >= 2:
                            pe.wait_ge(s_gz, b * NT + t - 1)
                        for c in range(KC):
                            last = nc.tensor.matmul(ps[:, 6 + t % 2, :], core.xnT[:, c, t * P:(t + 1) * P],
                                                    w["mb_win"][:, c, MB_E:2 * MB_E], start=(c == 0), stop=(c == KC - 1))
                        last.then_inc(s_z, 1)
                    for k, key in enumerate(("mb_wdt", "mb_wb", "mb_wc")):
                        for m in range(MB_EC):
                            if k == 0:
                                pe.wait_ge(s_u, b * MB_EC + m + 1)
                            last = nc.tensor.matmul(ps[:, 2 + k, :], w[key][:, m, :], uT[:, m, :],
                                                    start=(m == 0), stop=(m == MB_EC - 1))
                        last.then_inc(s_dbc, 1)
                    pe.wait_ge(s_gz, b * NT + NT)
                    for t in range(NT):
                        bank = (5, 6, 7, 5)[t]
                        if t == 3:
                            pe.wait_ge(s_ut, b * NT + 1)
                        for m in range(MB_EC):
                            last = nc.tensor.transpose(ps[:, bank, m * P:(m + 1) * P], uT[:, m, t * P:(t + 1) * P],
                                                       core.ident[:, :])
                        last.then_inc(s_utp, 1)
                    pe.wait_ge(s_cf, b + 1)
                    for t in range(NT):
                        last = nc.tensor.matmul(ps[:, 0, t:t + 1], cdp[:, t * P:(t + 1) * P], w["mb_one"][:, :],
                                                start=True, stop=True)
                    last.then_inc(s_cd, 1)
                    for t in range(NT):
                        last = nc.tensor.transpose(ps[:, 1, t * P:(t + 1) * P], bs[:, t * P:(t + 1) * P],
                                                   core.ident[:, :])
                    last.then_inc(s_bstp, 1)
                    pe.wait_ge(s_bst, b + 1)
                    pe.wait_ge(s_ut, b * NT + NT)

                    def pairs(i):
                        if i >= 1:
                            pe.wait_ge(s_m, b * NT + i)
                        for g, n in ((0, 4), (1, MB_LV - 4)):
                            last = nc.tensor.matmul(ps[:, 2 + g, 0:n * P], bs[:, i * P:(i + 1) * P],
                                                    cfm[:, 4 * g:4 * g + n, i * P:(i + 1) * P], start=True, stop=True)
                        last.then_inc(s_p, 1)
                        if i < NT - 1:
                            if i >= 1:
                                pe.wait_ge(s_h, b * (NT - 1) + i)
                            nc.tensor.matmul(ps[:, 4, :], bst[:, i, :], ut[:, i, :],
                                             start=True, stop=True).then_inc(s_hp, 1)

                    pairs(0)
                    for i in range(NT):
                        if i + 1 < NT:
                            pairs(i + 1)
                        pe.wait_ge(s_m, b * NT + i + 1)
                        if i >= 2:
                            pe.wait_ge(s_y, b * NT + i - 1)
                        last = nc.tensor.matmul(ps[:, 6 + i % 2, :], ms[:, i % 2, :], ut[:, i, :],
                                                start=True, stop=(i == 0))
                        if i:
                            pe.wait_ge(s_h, b * (NT - 1) + i)
                            last = nc.tensor.matmul(ps[:, 6 + i % 2, :], cfm[:, 7, i * P:(i + 1) * P],
                                                    hs[:, (i - 1) % 2, :], start=False, stop=True)
                        last.then_inc(s_yp, 1)
                    pe.wait_ge(s_y, b * NT + NT)
                    for m in range(MB_EC):
                        for t in range(NT):
                            last = nc.tensor.transpose(ps[:, 2 + m, t * P:(t + 1) * P], gz[:, t, m * P:(m + 1) * P],
                                                       core.ident[:, :])
                        last.then_inc(s_yTp, 1)
                    pe.wait_ge(s_yT, b * MB_EC + MB_EC)
                    for t in range(NT):
                        for m in range(MB_EC):
                            last = nc.tensor.matmul(ps[:, 6 + t // 2, (t % 2) * C:(t % 2 + 1) * C],
                                                    yT[:, m, t * P:(t + 1) * P], w["mb_wout"][:, m, :],
                                                    start=(m == 0), stop=(m == MB_EC - 1))
                    last.then_inc(s_o, 1)

            @block.scalar
            def _(act):
                std_of_tokens(core, act, s_std)
                act.wait_ge(core.loaded["mb"], core.loads["mb"])
                nc.scalar.activation(na[:, :], w["mb_alog"][:, :], ACT.Exp).then_inc(s_A, 1)
                with act.Fori(0, B) as b:
                    act.wait_ge(s_xT, b + 1)
                    nc.scalar.copy(core.xnT[:, :, :], ps[:, 0:2, :]).then_inc(s_xnT, 1)
                    for m in range(MB_EC):
                        act.wait_ge(s_xi, b * MB_EC + m + 1)
                        nc.scalar.copy(xi[:, m, HALO:HALO + T], ps[:, 2 + m, :]).then_inc(s_xic, 1)
                    for t in range(NT):
                        act.wait_ge(s_z, b * NT + t + 1)
                        nc.scalar.activation(gz[:, t, :], ps[:, 6 + t % 2, :], ACT.Silu).then_inc(s_gz, 1)
                    for m in range(MB_EC):
                        act.wait_ge(s_cv, b * MB_EC + m + 1)
                        nc.scalar.activation(uT[:, m, :], cv[:, m, :], ACT.Silu,
                                             bias=w["mb_cb"][:, m:m + 1]).then_inc(s_u, 1)
                    act.wait_ge(s_dbc, b * 3 + 1)
                    nc.scalar.activation(ax[:, :], ps[:, 2, :], ACT.Abs, bias=w["mb_bdt"][:, :])
                    nc.scalar.activation(rl[:, :], ps[:, 2, :], ACT.Relu, bias=w["mb_bdt"][:, :])
                    act.drain()
                    nc.scalar.activation(ex[:, :], ax[:, :], ACT.Exp, scale=-1.0)
                    act.drain()
                    nc.scalar.activation(lp[:, :], ex[:, :], ACT.Ln, bias=core.one[:, :]).then_inc(s_ln, 1)
                    act.wait_ge(s_delta, b + 1)
                    nc.scalar.activation(dA[:, 1:T + 1], delta[:, :], ACT.Exp, scale=na[:, :]).then_inc(s_dA, 1)
                    for t in range(NT):
                        act.wait_ge(s_utp, b * NT + t + 1)
                        nc.scalar.copy(ut[:, t, :], ps[:, (5, 6, 7, 5)[t], :]).then_inc(s_ut, 1)
                    act.wait_ge(s_bstp, b + 1)
                    nc.scalar.copy(bst[:, :, :], ps[:, 1, :].rearrange("p (t q) -> p t q", t=NT)).then_inc(s_bst, 1)
                    for m in range(MB_EC):
                        act.wait_ge(s_yTp, b * MB_EC + m + 1)
                        nc.scalar.copy(yT[:, m, :], ps[:, 2 + m, :]).then_inc(s_yT, 1)

            @block.vector
            def _(dve):
                nc.vector.memset(xi[:, :, 0:HALO], 0.0)
                nc.vector.memset(dA[:, :], 1.0)
                rstd_of_tokens(core, dve, s_std)
                dve.wait_ge(s_A, 1)
                nc.vector.tensor_scalar(na[:, :], na[:, :], -1.0, None, ALU.mult)
                dve.drain()
                with dve.Fori(0, B) as b:
                    normalise(core, dve, b, s_xn)
                    for m in range(MB_EC):
                        dve.wait_ge(s_xic, b * MB_EC + m + 1)
                        nc.vector.tensor_scalar(cv[:, m, :], xi[:, m, 0:T], w["mb_cw"][:, m, 0:1], None, ALU.mult)
                        for k in range(1, MB_TAPS):
                            dve.drain()
                            last = nc.vector.scalar_tensor_tensor(cv[:, m, :], xi[:, m, k:k + T],
                                                                  w["mb_cw"][:, m, k:k + 1], cv[:, m, :],
                                                                  ALU.mult, ALU.add)
                        last.then_inc(s_cv, 1)
                    dve.wait_ge(s_ln, b + 1)
                    nc.vector.tensor_tensor(delta[:, :], rl[:, :], lp[:, :], ALU.add).then_inc(s_delta, 1)
                    dve.drain()
                    dve.wait_ge(s_dbc, b * 3 + 3)
                    nc.vector.tensor_tensor(dB[:, :], delta[:, :], ps[:, 3, :], ALU.mult)
                    dve.drain()
                    nc.vector.tensor_tensor(cdp[:, :], dB[:, :], ps[:, 4, :], ALU.mult)
                    dve.wait_ge(s_dA, b + 1)
                    nc.vector.tensor_tensor_scan(fw[:, :], dA[:, 0:T], w["mb_rf"][:, :], 0.0, ALU.mult, ALU.max)
                    nc.vector.tensor_tensor_scan(bw[:, ::-1], dA[:, 2:T + 2][:, ::-1], w["mb_rb"][:, ::-1], 0.0,
                                                 ALU.mult, ALU.max)
                    dve.drain()
                    nc.vector.tensor_tensor(fw[:, :], fw[:, :], dA[:, 1:T + 1], ALU.mult)
                    nc.vector.tensor_tensor(bs[:, :], bw[:, :], dB[:, :], ALU.mult)
                    dve.drain()
                    nc.vector.tensor_tensor(cf[:, :], fw[:, :], ps[:, 4, :], ALU.mult)
                    dve.drain()
                    for g in range(8):
                        last = nc.vector.tensor_scalar(cfm[:, g, :], cf[:, :], w["mb_group"][:, g:g + 1], None, ALU.mult)
                    last.then_inc(s_cf, 1)
                    dve.wait_ge(s_cd, b + 1)
                    nc.vector.tensor_copy(cd[:, :], ps[:, 0, 0:NT])

                    def tile_m(i):
                        dve.wait_ge(s_p, b * NT + i + 1)
                        if i >= 2:
                            dve.wait_ge(s_yp, b * NT + i - 1)
                        nc.vector.tensor_tensor(mm[:, :, :], ps[:, 2:4, :].rearrange("p a (l t) -> p (a l) t", t=P)[:, 0:MB_LV, :],
                                                w["mb_pairs"][:, :, :], ALU.mult)
                        dve.drain()
                        nc.vector.reduce_sum(ms[:, i % 2, :], mm[:, :, :].rearrange("p l t -> p t l"),
                                             axis=AX.X).then_inc(s_m, 1)

                    tile_m(0)
                    for i in range(NT):
                        if i < NT - 1:
                            dve.wait_ge(s_hp, b * (NT - 1) + i + 1)
                            if i == 0:
                                nc.vector.tensor_copy(hs[:, 0, :], ps[:, 4, :]).then_inc(s_h, 1)
                            else:
                                nc.vector.scalar_tensor_tensor(hs[:, i % 2, :], hs[:, (i - 1) % 2, :],
                                                               fw[:, i * P + P - 1:i * P + P], ps[:, 4, :],
                                                               ALU.mult, ALU.add).then_inc(s_h, 1)
                            tile_m(i + 1)
                        nc.vector.scalar_tensor_tensor(v1[:, i % 2, :], w["mb_d"][:, :], cd[:, i:i + 1], ut[:, i, :],
                                                       ALU.add, ALU.mult)
                        dve.drain()
                        dve.wait_ge(s_yp, b * NT + i + 1)
                        nc.vector.tensor_tensor(v1[:, i % 2, :], v1[:, i % 2, :], ps[:, 6 + i % 2, :], ALU.add)
                        dve.drain()
                        nc.vector.tensor_tensor(gz[:, i, :], gz[:, i, :], v1[:, i % 2, :], ALU.mult).then_inc(s_y, 1)
                    dve.wait_ge(s_o, b + 1)
                    add_to_residual(core, dve, b, ps[:, 6:8, :].rearrange("p a (t c) -> p (a t) c", t=2))
                    dve.drain()


F4_I = 704
F4_IC = -(-F4_I // P)
F4_BLK = 16
F4_H = F4_I // 2


def fp4_round(core, dve, x, sc, inv, av, q, width):
    nc = core.nc
    blocks = lambda a: a.rearrange("p n (k e) -> p (n k) e", e=F4_BLK)
    dve.drain()
    nc.vector.tensor_reduce(sc, blocks(x), op=ALU.max, axis=AX.X, apply_absolute_value=True)
    dve.drain()
    nc.vector.tensor_scalar(sc, sc, 1.0 / 6.0, 1e-12, ALU.mult, ALU.max)
    dve.drain()
    nc.vector.reciprocal(inv, sc)
    dve.drain()
    nc.vector.tensor_tensor(blocks(av), blocks(x), bcast(inv, 2, F4_BLK), ALU.mult)
    dve.drain()
    nc.vector.tensor_scalar(av.bitcast(U32), av.bitcast(U32), 0x7FFFFFFF, None, ALU.bitwise_and)
    dve.drain()
    nc.vector.tensor_scalar(q, av, 5.0, 2.0, ALU.is_gt, ALU.mult)
    for mid in (3.5, 2.5):
        dve.drain()
        nc.vector.scalar_tensor_tensor(q, av, mid, q, ALU.is_gt, ALU.add)
    dve.drain()
    nc.vector.tensor_scalar(q, q, 2.0, None, ALU.mult)
    for mid in (1.75, 1.25, 0.75, 0.25):
        dve.drain()
        nc.vector.scalar_tensor_tensor(q, av, mid, q, ALU.is_gt, ALU.add)
    dve.drain()
    nc.vector.tensor_scalar(x.bitcast(U32), x.bitcast(U32), 0x80000000, None, ALU.bitwise_and)
    nc.vector.tensor_scalar(sc, sc, 0.5, None, ALU.mult)
    dve.drain()
    nc.vector.tensor_tensor(x.bitcast(U32), x.bitcast(U32), q.bitcast(U32), ALU.bitwise_or)
    dve.drain()
    return nc.vector.tensor_tensor(blocks(x), blocks(x), bcast(sc, 2, F4_BLK), ALU.mult)


def fp4_weights(core, w, space, tag):
    nc, ps = core.nc, core.ps
    for key, shape in (("f4_gT", [P, KC, F4_I]), ("f4_uT", [P, KC, F4_I]), ("f4_dT", [P, F4_IC, C])):
        w[key] = space.enter_context(nc.sbuf_tensor("w_" + key, shape, F32))
    ctx = ExitStack()
    own = Semaphores(nc)
    with own, ctx:
        def sb(name, shape, dt=F32):
            return ctx.enter_context(nc.sbuf_tensor("fw_" + name, shape, dt))

        def sem(name):
            return own.named("fw_" + name)

        n = F4_IC * C // F4_BLK
        sc, inv = sb("sc", [P, n]), sb("inv", [P, n])
        av, q = sb("av", [P, F4_IC * C]), sb("q", [P, F4_IC * C])
        s_q, s_tr, s_cp = sem("q"), sem("tr"), sem("cp")
        kinds = (("f4_wg", "f4_gT"), ("f4_wu", "f4_uT"), ("f4_wd", "f4_dT"))

        with nc.Block() as block:
            @block.vector
            def _(dve):
                dve.wait_ge(core.loaded["f4"], core.loads["f4"])
                for key, _ in kinds:
                    x = w[key][:, :, :]
                    m, width = x.shape[1], x.shape[2]
                    size = m * width
                    view = lambda a: a[:, 0:size].rearrange("p (m k) -> p m k", m=m)
                    k = size // F4_BLK
                    fp4_round(core, dve, x, sc[:, 0:k], inv[:, 0:k], view(av), view(q), width).then_inc(s_q, 1)

            @block.tensor
            def _(pe):
                done = 0
                for k, (key, _) in enumerate(kinds):
                    pe.wait_ge(s_q, k + 1)
                    rows = F4_IC if k < 2 else KC
                    for i in range(rows):
                        if done >= 8:
                            pe.wait_ge(s_cp, done - 7)
                        full = P if k == 2 or i < F4_IC - 1 else F4_I - i * P
                        cols = KC if k < 2 else 4
                        for c in range(cols):
                            last = nc.tensor.transpose(ps[:, done % 8, c * P:c * P + full],
                                                       w[key][0:full, i, c * P:(c + 1) * P],
                                                       core.ident[0:full, 0:full])
                        last.then_inc(s_tr, 1)
                        done += 1
                        if k == 2:
                            if done >= 8:
                                pe.wait_ge(s_cp, done - 7)
                            nc.tensor.transpose(ps[:, done % 8, 0:P], w[key][:, i, 4 * P:5 * P], core.ident[:, :])
                            nc.tensor.transpose(ps[0:64, done % 8, P:2 * P], w[key][:, i, 5 * P:F4_I],
                                                core.ident[:, :]).then_inc(s_tr, 1)
                            done += 1

            @block.scalar
            def _(act):
                done = 0
                for k, (_, key) in enumerate(kinds):
                    for i in range(F4_IC if k < 2 else KC):
                        act.wait_ge(s_tr, done + 1)
                        if k < 2:
                            full = P if i < F4_IC - 1 else F4_I - i * P
                            src = ps[:, done % 8, 0:2 * P].rearrange("p (c q) -> p c q", c=KC)[:, :, 0:full]
                            nc.scalar.copy(w[key][:, :, i * P:i * P + full], src).then_inc(s_cp, 1)
                            done += 1
                        else:
                            nc.scalar.copy(w[key][:, 0:4, i * P:(i + 1) * P],
                                           ps[:, done % 8, :].rearrange("p (c q) -> p c q", c=4)).then_inc(s_cp, 1)
                            done += 1
                            act.wait_ge(s_tr, done + 1)
                            nc.scalar.copy(w[key][:, 4, i * P:(i + 1) * P], ps[:, done % 8, 0:P])
                            nc.scalar.copy(w[key][0:64, 5, i * P:(i + 1) * P],
                                           ps[0:64, done % 8, P:2 * P]).then_inc(s_cp, 1)
                            done += 1


def fp4_ffn(core, w, tag):
    nc, ps = core.nc, core.ps
    ctx = ExitStack()
    own = Semaphores(nc)
    with own, ctx:
        def sb(name, shape, dt=F32):
            return ctx.enter_context(nc.sbuf_tensor(f"{tag}_" + name, shape, dt))

        def sem(name):
            return own.named(f"{tag}_" + name)

        nx, nh = NT * C // F4_BLK, 2 * F4_I // F4_BLK
        scx, invx = sb("scx", [P, nx]), sb("invx", [P, nx])
        avx, qx = sb("avx", [P, NT, C]), sb("qx", [P, NT, C])
        sg = sb("sg", [P, 2, F4_I])
        h = sb("h", [P, NT, F4_I])
        sch, invh = sb("sch", [P, nh]), sb("invh", [P, nh])
        avh, qh = sb("avh", [P, 2, F4_I]), sb("qh", [P, 2, F4_I])
        hT = sb("hT", [P, F4_IC, T])

        s_std, s_xn, s_xq, s_xT, s_xnT, s_gu, s_sg, s_h, s_hq, s_hTp, s_hT, s_y = (
            sem(x) for x in ("std", "xn", "xq", "xT", "xnT", "gu", "sg", "h", "hq", "hTp", "hT", "y"))

        with nc.Block() as block:
            @block.tensor
            def _(pe):
                with pe.Fori(0, B) as b:
                    pe.wait_ge(s_xq, b + 1)
                    transpose_tokens(core, core.xn, 4).then_inc(s_xT, 1)
                    pe.wait_ge(s_xnT, b + 1)
                    for t in range(NT):
                        if t >= 1:
                            pe.wait_ge(s_h, b * NT + t)
                        for k, key in enumerate(("f4_gT", "f4_uT")):
                            for half in range(2):
                                for c in range(KC):
                                    last = nc.tensor.matmul(ps[:, 2 * k + half, 0:F4_H],
                                                            core.xnT[:, c, t * P:(t + 1) * P],
                                                            w[key][:, c, half * F4_H:(half + 1) * F4_H],
                                                            start=(c == 0), stop=(c == KC - 1))
                        last.then_inc(s_gu, 1)
                    for pair in range(2):
                        pe.wait_ge(s_hq, b * 2 + pair + 1)
                        for g in range(3):
                            for m in (2 * g, 2 * g + 1):
                                size = min(P, F4_I - m * P)
                                for t in range(2):
                                    at = (m % 2) * 2 * P + t * P
                                    last = nc.tensor.transpose(ps[0:size, 4 + g, at:at + P],
                                                               h[:, 2 * pair + t, m * P:m * P + size],
                                                               core.ident[:, :])
                            last.then_inc(s_hTp, 1)
                        pe.wait_ge(s_hT, b * 6 + pair * 3 + 3)
                        for t in range(2 * pair, 2 * pair + 2):
                            for m in range(F4_IC):
                                size = min(P, F4_I - m * P)
                                last = nc.tensor.matmul(ps[:, 0 + pair, (t % 2) * C:(t % 2 + 1) * C],
                                                        hT[0:size, m, t * P:(t + 1) * P], w["f4_dT"][0:size, m, :],
                                                        start=(m == 0), stop=(m == F4_IC - 1))
                    last.then_inc(s_y, 1)

            @block.scalar
            def _(act):
                std_of_tokens(core, act, s_std)
                with act.Fori(0, B) as b:
                    act.wait_ge(s_xT, b + 1)
                    nc.scalar.copy(core.xnT[:, :, :], ps[:, 4:6, :]).then_inc(s_xnT, 1)
                    for t in range(NT):
                        act.wait_ge(s_gu, b * NT + t + 1)
                        nc.scalar.activation(sg[:, t % 2, :].rearrange("p (a n) -> p a n", a=2), ps[:, 0:2, 0:F4_H],
                                             ACT.Silu).then_inc(s_sg, 1)
                    for pair in range(2):
                        for g in range(3):
                            act.wait_ge(s_hTp, b * 6 + pair * 3 + g + 1)
                            cols = slice(2 * pair * P, (2 * pair + 2) * P)
                            if g < 2:
                                last = nc.scalar.copy(hT[:, 2 * g:2 * g + 2, cols],
                                                      ps[:, 4 + g, :].rearrange("p (m q) -> p m q", m=2))
                            else:
                                nc.scalar.copy(hT[:, 4, cols], ps[:, 6, 0:2 * P])
                                last = nc.scalar.copy(hT[0:64, 5, cols], ps[0:64, 6, 2 * P:4 * P])
                            last.then_inc(s_hT, 1)

            @block.vector
            def _(dve):
                rstd_of_tokens(core, dve, s_std)
                with dve.Fori(0, B) as b:
                    normalise(core, dve, b, s_xn)
                    fp4_round(core, dve, core.xn[:, :, :], scx[:, :], invx[:, :], avx[:, :, :], qx[:, :, :],
                              C).then_inc(s_xq, 1)
                    for t in range(NT):
                        dve.wait_ge(s_sg, b * NT + t + 1)
                        nc.vector.tensor_tensor(h[:, t, :].rearrange("p (a n) -> p a n", a=2),
                                                sg[:, t % 2, :].rearrange("p (a n) -> p a n", a=2),
                                                ps[:, 2:4, 0:F4_H], ALU.mult).then_inc(s_h, 1)
                    for pair in range(2):
                        fp4_round(core, dve, h[:, 2 * pair:2 * pair + 2, :], sch[:, :], invh[:, :], avh[:, :, :],
                                  qh[:, :, :], F4_I).then_inc(s_hq, 1)
                    dve.wait_ge(s_y, b + 1)
                    add_to_residual(core, dve, b, ps[:, 0:2, :].rearrange("p a (t c) -> p (a t) c", t=2))
                    dve.drain()


AB_H = 16
AB_D = C // AB_H


def full_attention(core, w):
    nc, ps = core.nc, core.ps
    HC = P // AB_D
    NI = AB_H * NT
    NQ = AB_H // 4
    ctx = ExitStack()
    own = Semaphores(nc)
    with own, ctx:
        def sb(name, shape, dt=F32):
            return ctx.enter_context(nc.sbuf_tensor("ab_" + name, shape, dt))

        def sem(name):
            return own.named("ab_" + name)

        kT = sb("kT", [P, KC, T])
        qm = sb("qm", [P, AB_H, T])
        vx = sb("vx", [P, NT, AB_H, 32])
        nmx = sb("nmx", [P, 4])
        pq = sb("pq", [P, 4, T])
        pt = sb("pt", [P, 4, NT, T])
        qb = pq[:, 0:2, :]
        rot = pq[:, 2:4, :]
        qk = pt[:, 0, :, :]
        osb = sb("osb", [P, T])
        rr = sb("rr", [P, NT, 4])
        att = core.xn[:, :, :].rearrange("p t (h d) -> p t h d", d=AB_D)
        outT = kT

        s_std, s_xn, s_xT, s_xnT, s_qk, s_v, s_rot, s_qkT, s_kT, s_qmA, s_qmD, s_vx = (
            sem(x) for x in ("std", "xn", "xT", "xnT", "qk", "v", "rot", "qkT", "kT", "qmA", "qmD", "vx"))
        s_s, s_mx, s_e, s_tp, s_tA, s_tD, s_av, s_osb, s_oT, s_att, s_attT, s_outT, s_y = (
            sem(x) for x in ("s", "mx", "e", "tp", "tA", "tD", "av", "osb", "oT", "att", "attT", "outT", "y"))

        with nc.Block() as block:
            @block.tensor
            def _(pe):
                with pe.Fori(0, B) as b:
                    pe.wait_ge(s_xn, b + 1)
                    transpose_tokens(core, core.xn, 0).then_inc(s_xT, 1)
                    pe.wait_ge(s_xnT, b + 1)
                    for t in range(NT):
                        for c in range(KC):
                            last = nc.tensor.matmul(ps[:, 2 + t, :], core.xnT[:, c, t * P:(t + 1) * P],
                                                    w["ab_wqk"][:, c, :], start=(c == 0), stop=(c == KC - 1))
                        last.then_inc(s_qk, 1)
                    for t in range(NT):
                        for c in range(KC):
                            last = nc.tensor.matmul(ps[:, 6 + t // 2, (t % 2) * C:(t % 2 + 1) * C],
                                                    core.xnT[:, c, t * P:(t + 1) * P],
                                                    w["ab_wv"][:, c, :], start=(c == 0), stop=(c == KC - 1))
                    last.then_inc(s_v, 1)
                    pe.wait_ge(s_rot, b + 1)
                    for ch in range(2 * KC):
                        for t in range(NT):
                            last = nc.tensor.transpose(ps[:, 2 + ch, t * P:(t + 1) * P],
                                                       qk[:, t, ch * P:(ch + 1) * P], core.ident[:, :])
                        last.then_inc(s_qkT, 1)
                    pe.wait_ge(s_kT, b + 1)
                    pe.wait_ge(s_qmA, b + 1)
                    pe.wait_ge(s_qmD, b + 1)
                    pe.wait_ge(s_vx, b + 1)

                    def scores(n):
                        h, qt = n // NT, n % NT
                        if n >= 4:
                            pe.wait_ge(s_e, b * NI + n - 3)
                        nc.tensor.matmul(ps[:, 2 + n % 4, :], qm[:, h, qt * P:(qt + 1) * P], kT[:, h // HC, :],
                                         start=True, stop=True).then_inc(s_s, 1)

                    def turn(n):
                        pe.wait_ge(s_e, b * NI + n + 1)
                        if n >= 2 and n % 2 == 0:
                            pe.wait_ge(s_tA, b * NI // 2 + n // 2)
                        if n >= 2 and n % 2 == 1:
                            pe.wait_ge(s_tD, b * NI // 2 + n // 2)
                        for j in range(NT):
                            last = nc.tensor.transpose(ps[:, n % 2, j * P:(j + 1) * P],
                                                       pq[:, n % 4, j * P:(j + 1) * P], core.ident[:, :])
                        last.then_inc(s_tp, 1)

                    def values(g):
                        pe.wait_ge(s_tA, b * NI // 2 + 8 * g + 8)
                        pe.wait_ge(s_tD, b * NI // 2 + 8 * g + 8)
                        if g >= 1:
                            pe.wait_ge(s_osb, b * NQ + g)
                        for j in range(NT):
                            for i in range(4):
                                last = nc.tensor.matmul(ps[32 * i:32 * i + 32, 6, :], vx[:, j, 4 * g + i, :],
                                                        pt[:, i, j, :], start=(j == 0), stop=(j == NT - 1))
                        last.then_inc(s_av, 1)

                    def back(g):
                        pe.wait_ge(s_osb, b * NQ + g + 1)
                        if g >= 1:
                            pe.wait_ge(s_att, b * NQ + g)
                        for t in range(NT):
                            last = nc.tensor.transpose(ps[:, 7, t * P:(t + 1) * P], osb[:, t * P:(t + 1) * P],
                                                       core.ident[:, :])
                        last.then_inc(s_oT, 1)

                    for n in range(3):
                        scores(n)
                    for n in range(NI + 7):
                        if n + 3 < NI:
                            scores(n + 3)
                        if n < NI:
                            turn(n)
                        g, k = (n - 17) // 16, (n - 17) % 16
                        if k == 0 and g >= 0:
                            values(g)
                        if n >= 17 and k == 5:
                            back(g)
                    pe.wait_ge(s_att, b * NQ + NQ)
                    for c in range(KC):
                        for t in range(NT):
                            last = nc.tensor.transpose(ps[:, c, t * P:(t + 1) * P],
                                                       att[:, t, 8 * c:8 * c + 8, :], core.ident[:, :])
                    last.then_inc(s_attT, 1)
                    pe.wait_ge(s_outT, b + 1)
                    for t in range(NT):
                        bank = ps[:, 2 + t // 2, (t % 2) * C:(t % 2 + 1) * C]
                        for c in range(KC):
                            nc.tensor.matmul(bank, outT[:, c, t * P:(t + 1) * P], w["ab_wo"][:, c, :],
                                             start=(c == 0), stop=False)
                        last = nc.tensor.matmul(bank, w["ab_ones"][:, :], w["ab_bo"][:, :], start=False, stop=True)
                    last.then_inc(s_y, 1)

            @block.scalar
            def _(act):
                std_of_tokens(core, act, s_std)
                with act.Fori(0, B) as b:
                    act.wait_ge(s_xT, b + 1)
                    nc.scalar.copy(core.xnT[:, :, :], ps[:, 0:2, :]).then_inc(s_xnT, 1)
                    act.wait_ge(s_qkT, b * 4 + 1)
                    for h in range(HC):
                        last = nc.scalar.mul(qm[:, h, :], ps[:, 2, :], w["ab_hmask"][:, h:h + 1])
                    last.then_inc(s_qmA, 1)
                    act.wait_ge(s_qkT, b * 4 + 4)
                    nc.scalar.copy(kT[:, :, :], ps[:, 4:6, :]).then_inc(s_kT, 1)
                    for n in range(NI + 10):
                        if n < NI:
                            act.wait_ge(s_mx, b * NI + n + 1)
                            if n >= 4:
                                act.wait_ge(s_tp, b * NI + n - 3)
                            nc.scalar.activation(pq[:, n % 4, :], ps[:, 2 + n % 4, :], ACT.Exp,
                                                 bias=nmx[:, n % 4:n % 4 + 1]).then_inc(s_e, 1)
                        m = n - 2
                        if 0 <= m < NI and m % 2 == 0:
                            act.wait_ge(s_tp, b * NI + m + 1)
                            if m >= 16 and m % 16 == 0:
                                act.wait_ge(s_av, b * NQ + m // 16)
                            h, qt = m // NT, m % NT
                            nc.scalar.copy(pt[:, h % 4, :, qt * P:(qt + 1) * P],
                                           ps[:, 0, :].rearrange("p (j q) -> p j q", j=NT)).then_inc(s_tA, 1)
                        g, k = (n - 20) // 16, (n - 20) % 16
                        if k == 0 and 0 <= g < NQ:
                            act.wait_ge(s_av, b * NQ + g + 1)
                            if g >= 1:
                                act.wait_ge(s_oT, b * NQ + g)
                            nc.scalar.copy(osb[:, :], ps[:, 6, :]).then_inc(s_osb, 1)
                    act.wait_ge(s_attT, b + 1)
                    nc.scalar.copy(outT[:, :, :], ps[:, 0:2, :]).then_inc(s_outT, 1)

            @block.vector
            def _(dve):
                nc.vector.memset(vx[:, :, :, 16:17], 1.0)
                nc.vector.memset(vx[:, :, :, 17:32], 0.0)
                rstd_of_tokens(core, dve, s_std)
                with dve.Fori(0, B) as b:
                    normalise(core, dve, b, s_xn)
                    for t in range(NT):
                        dve.wait_ge(s_qk, b * NT + t + 1)
                        x, r = qb[:, t % 2, :], rot[:, t % 2, :]
                        nc.vector.tensor_tensor(x, ps[:, 2 + t, :], w["ab_bqk"][:, :], ALU.add)
                        dve.drain()
                        halves = x.rearrange("p (h a d) -> p h a d", a=2, d=AB_D // 2)
                        nc.vector.tensor_tensor(r.rearrange("p (h a d) -> p h a d", a=2, d=AB_D // 2),
                                                halves[:, :, ::-1, :], bcast(w["ab_sin"][:, t, :, :], 1, 2 * AB_H),
                                                ALU.mult)
                        nc.vector.tensor_tensor(qk[:, t, :].rearrange("p (h d) -> p h d", d=AB_D),
                                                x.rearrange("p (h d) -> p h d", d=AB_D),
                                                bcast(w["ab_cos"][:, t, :], 1, 2 * AB_H), ALU.mult)
                        dve.drain()
                        nc.vector.tensor_tensor(qk[:, t, :], qk[:, t, :], r, ALU.add)
                    dve.drain().then_inc(s_rot, 1)
                    dve.wait_ge(s_v, b + 1)
                    for t in range(NT):
                        last = nc.vector.tensor_tensor(
                            vx[:, t, :, 0:16],
                            ps[:, 6 + t // 2, (t % 2) * C:(t % 2 + 1) * C].rearrange("p (h d) -> p h d", d=AB_D),
                            w["ab_bv"][:, :].rearrange("p (h d) -> p h d", d=AB_D), ALU.add)
                    last.then_inc(s_vx, 1)
                    dve.wait_ge(s_qkT, b * 4 + 2)
                    for h in range(HC):
                        last = nc.vector.tensor_scalar(qm[:, HC + h, :], ps[:, 3, :], w["ab_hmask"][:, h:h + 1],
                                                       None, ALU.mult)
                    last.then_inc(s_qmD, 1)
                    for n in range(NI + 10):
                        if n < NI:
                            dve.wait_ge(s_s, b * NI + n + 1)
                            if n >= 4:
                                dve.wait_ge(s_e, b * NI + n - 3)
                            nc.vector.tensor_reduce(nmx[:, n % 4:n % 4 + 1], ps[:, 2 + n % 4, :], op=ALU.max,
                                                    axis=AX.X, negate=True).then_inc(s_mx, 1)
                        m = n - 3
                        if 0 <= m < NI and m % 2 == 1:
                            dve.wait_ge(s_tp, b * NI + m + 1)
                            if m > 16 and m % 16 == 1:
                                dve.wait_ge(s_av, b * NQ + m // 16)
                            h, qt = m // NT, m % NT
                            nc.vector.tensor_copy(pt[:, h % 4, :, qt * P:(qt + 1) * P],
                                                  ps[:, 1, :].rearrange("p (j q) -> p j q", j=NT)).then_inc(s_tD, 1)
                        g, k = (n - 25) // 16, (n - 25) % 16
                        if k == 0 and 0 <= g < NQ:
                            dve.wait_ge(s_oT, b * NQ + g + 1)
                            sums = ps[:, 7, :].rearrange("p (t h d) -> p t h d", t=NT, h=4)
                            nc.vector.reciprocal(rr[:, :, :], sums[:, :, :, 16])
                            dve.drain()
                            nc.vector.tensor_tensor(att[:, :, 4 * g:4 * g + 4, :], sums[:, :, :, 0:16],
                                                    bcast(rr[:, :, :], 3, 16), ALU.mult).then_inc(s_att, 1)
                    dve.wait_ge(s_y, b + 1)
                    add_to_residual(core, dve, b, ps[:, 2:4, :].rearrange("p a (t c) -> p (a t) c", t=2))
                    dve.drain()


def network(nc, a, out, stages=range(1, 9)):
    ctx = ExitStack()
    with ctx:
        core = Core(nc, ctx)
        core.eps = ctx.enter_context(nc.sbuf_tensor("ln_eps", [P, 1], F32))
        core.rms_eps = ctx.enter_context(nc.sbuf_tensor("rms_eps", [P, 1], F32))
        core.one = ctx.enter_context(nc.sbuf_tensor("one", [P, 1], F32))
        core.loaded, core.loads, w = {}, {}, {}
        s_x = ctx.enter_context(nc.semaphore("x_loaded"))
        s_out = ctx.enter_context(nc.semaphore("out_stored"))
        x_v = a["x"].rearrange("b (t p) c -> p b t c", p=P)
        out_v = out.rearrange("b (t p) c -> p b t c", p=P)

        def group(name, space, items):
            if name not in core.loaded:
                core.loaded[name] = ctx.enter_context(nc.semaphore(f"{name}_loaded"))
                core.loads[name] = 0
            moves = []
            for key, src in items:
                w[key] = space.enter_context(nc.sbuf_tensor("w_" + key, list(src.shape), F32))
                dst = w[key][tuple([slice(None)] * len(src.shape))]
                moves.append((dst, src))
            core.loads[name] += 16 * len(moves)
            return name, moves

        def issue(eng, what):
            name, moves = what
            for dst, src in moves:
                eng.dma_start(dst, src).then_inc(core.loaded[name], 16)

        early = ExitStack()
        da = group("da", early, [
            ("da_wqk", a["da_wqk"].rearrange("(c p) n -> p c n", p=P)),
            ("da_wv", a["da_wv"].rearrange("(c p) n -> p c n", p=P)),
            ("da_wo", a["da_wo"].rearrange("(c p) n -> p c n", p=P)),
            ("da_lq", a["da_lq"].partition_broadcast(P)),
            ("da_lk", a["da_lk"].partition_broadcast(P)),
            ("da_hmask", a["da_hmask"]), ("da_tri", a["da_tri"]), ("da_cos", a["da_cos"]), ("da_sin", a["da_sin"])])

        with nc.Block() as block:
            @block.sync
            def _(sp):
                with nc.allow_non_contiguous_dma(reason="small tables"):
                    for b in range(B):
                        sp.dma_start(core.res[:, b, :, :], x_v[:, b, :, :]).then_inc(s_x, 16)
                    sp.dma_start(core.ident[:, :], a["ident"]).then_inc(s_x, 16)
                    issue(sp, da)

            @block.vector
            def _(dve):
                nc.vector.memset(core.eps[:, :], LN_EPS)
                nc.vector.memset(core.rms_eps[:, :], RMS_EPS)
                nc.vector.memset(core.one[:, :], 1.0)
                dve.wait_ge(s_x, 16 * (B + 1))
                with dve.Fori(0, B) as b:
                    token_stats(core, dve, b)
                    dve.drain()
                dve.wait_ge(core.loaded["da"], core.loads["da"])

        if 1 in stages:
            diff_attention(core, w)
        early.close()

        layer0 = ExitStack()
        moe_small = group("moe", layer0, [
            ("moe_router", a["moe_router"].rearrange("(c p) n -> p c n", p=P)),
            ("moe_rb", a["moe_rb"].partition_broadcast(P)),
            ("moe_iota", a["moe_iota"].partition_broadcast(P)),
            ("moe_b1", a["moe_b1"].rearrange("e (m p) -> p e m", p=P)),
            ("moe_b2", a["moe_b2"])])
        lb = group("lb", layer0, [
            ("lb_wqkv", a["lb_wqkv"].rearrange("(c p) n -> p c n", p=P)),
            ("lb_wqh", a["lb_wqh"].rearrange("(c p) n -> p c n", p=P)),
            ("lb_wkvh", a["lb_wkvh"].rearrange("(c p) n -> p c n", p=P)),
            ("lb_woh", a["lb_woh"].rearrange("(c p) n -> p c n", p=P)),
            ("lb_wol", a["lb_wol"].rearrange("(c p) n -> p c n", p=P)),
            ("lb_lng", a["lb_lng"].rearrange("(c p) -> p c", p=P)),
            ("lb_lnb", a["lb_lnb"].rearrange("(c p) -> p c", p=P)),
            ("lb_gamma", a["lb_gamma"].rearrange("(c p) -> p c", p=P)),
            ("lb_rt", a["lb_rt"].rearrange("r (c p) -> p r c", p=P)),
            ("lb_iota", a["lb_iota"].partition_broadcast(P)),
            ("lb_hmask", a["lb_hmask"]), ("lb_later", a["lb_later"]), ("lb_place", a["lb_place"]),
            ("lb_mask", a["lb_mask"])])
        with nc.Block() as block:
            @block.sync
            def _(sp):
                with nc.allow_non_contiguous_dma(reason="small tables"):
                    issue(sp, moe_small)
                    issue(sp, lb)
                sp.wait_ge(core.loaded["moe"], core.loads["moe"])
        if 2 in stages:
            experts(core, w, a, "moe_a")
        if 3 in stages:
            routed_attention(core, w)
        if 4 in stages:
            experts(core, w, a, "moe_b")

        layer0.close()

        layer1 = ExitStack()
        mb = group("mb", layer1, [
            ("mb_win", a["mb_win"].rearrange("(c p) n -> p c n", p=P)),
            ("mb_wdt", a["mb_wdt"].rearrange("(c p) n -> p c n", p=P)),
            ("mb_wb", a["mb_wb"].rearrange("(c p) n -> p c n", p=P)),
            ("mb_wc", a["mb_wc"].rearrange("(c p) n -> p c n", p=P)),
            ("mb_wout", a["mb_wout"].rearrange("(c p) n -> p c n", p=P)),
            ("mb_cw", a["mb_cw"].rearrange("(c p) k -> p c k", p=P)),
            ("mb_cb", a["mb_cb"].rearrange("(c p) -> p c", p=P)),
            ("mb_d", a["mb_d"].partition_broadcast(P)),
            ("mb_bdt", a["mb_bdt"]), ("mb_alog", a["mb_alog"]), ("mb_group", a["mb_group"]), ("mb_one", a["mb_one"]),
            ("mb_rf", a["mb_rf"]), ("mb_rb", a["mb_rb"]), ("mb_pairs", a["mb_pairs"])])
        f4 = group("f4", layer1, [
            ("f4_wg", a["f4_wg"].rearrange("(m p) k -> p m k", p=P)),
            ("f4_wu", a["f4_wu"].rearrange("(m p) k -> p m k", p=P)),
            ("f4_wd", a["f4_wd"].rearrange("(m p) k -> p m k", p=P))])
        ab = group("ab", layer1, [
            ("ab_wqk", a["ab_wqk"].rearrange("(c p) n -> p c n", p=P)),
            ("ab_wv", a["ab_wv"].rearrange("(c p) n -> p c n", p=P)),
            ("ab_wo", a["ab_wo"].rearrange("(c p) n -> p c n", p=P)),
            ("ab_bqk", a["ab_bqk"].partition_broadcast(P)), ("ab_bv", a["ab_bv"].partition_broadcast(P)),
            ("ab_bo", a["ab_bo"]), ("ab_ones", a["ab_ones"]),
            ("ab_hmask", a["ab_hmask"]), ("ab_cos", a["ab_cos"]), ("ab_sin", a["ab_sin"])])
        with nc.Block() as block:
            @block.sync
            def _(sp):
                with nc.allow_non_contiguous_dma(reason="small tables"):
                    issue(sp, ab)
                    issue(sp, mb)
                    issue(sp, f4)
                sp.wait_ge(core.loaded["mb"], core.loads["mb"])
                sp.wait_ge(core.loaded["ab"], core.loads["ab"])

        if 5 in stages:
            state_space(core, w)
        fp4_weights(core, w, layer1, "fw")
        if 6 in stages:
            fp4_ffn(core, w, "f4a")
        if 7 in stages:
            full_attention(core, w)
        if 8 in stages:
            fp4_ffn(core, w, "f4b")

        with nc.Block() as block:
            @block.sync
            def _(sp):
                for g, n in core.loads.items():
                    sp.wait_ge(core.loaded[g], n)
                sp.dma_start(out_v, core.res[:, :, :, :]).then_inc(s_out, 16)
                sp.wait_ge(s_out, 16)
        layer1.close()


def layout(x):
    cat = np.concatenate
    f = np.float32
    a = {"x": x["L0_attn_a_x"]}
    a["da_wqk"] = cat([x["L0_attn_a_Wq"].T, x["L0_attn_a_Wk"].T], 1)
    a["da_wv"] = x["L0_attn_a_Wv"].T
    a["da_wo"] = x["L0_attn_a_Wproj"].T
    a["da_lq"] = np.stack([x["L0_attn_a_lq1"], x["L0_attn_a_lq2"]])
    a["da_lk"] = np.stack([x["L0_attn_a_lk1"], x["L0_attn_a_lk2"]])
    a["ident"] = np.eye(P, dtype=f)
    heads = P // DA_D
    a["da_hmask"] = (np.arange(P)[:, None] // DA_D == np.arange(heads)[None]).astype(f)

    a["da_tri"] = (np.arange(P)[:, None] <= np.arange(P)[None]).astype(f)

    def angles(theta, dim):
        inv = 1.0 / theta ** (np.arange(0, dim, 2, dtype=f) / dim)
        ang = np.outer(np.arange(T, dtype=f), inv.astype(f)).astype(f)
        ang = ang.reshape(NT, P, dim // 2).transpose(1, 0, 2)
        return np.cos(ang).astype(f), np.sin(ang).astype(f)

    cos, sin = angles(10000.0, DA_D)
    a["da_cos"] = cat([cos, cos], 2)
    a["da_sin"] = np.stack([sin, -sin], 2)
    a["moe_router"] = x["L0_ffn_router_w"]
    a["moe_rb"] = x["L0_ffn_router_b"]
    a["moe_iota"] = np.arange(NE, dtype=f)
    a["moe_b1"] = cat([x["L0_ffn_rb1"], x["L0_ffn_sb1"][None]])
    a["moe_b2"] = cat([x["L0_ffn_rb2"], x["L0_ffn_sb2"][None]])
    a["moe_w1"] = cat([x["L0_ffn_rw1"], x["L0_ffn_sw1"][None]])
    a["moe_w2"] = cat([x["L0_ffn_rw2"], x["L0_ffn_sw2"][None]])
    a["lb_wqkv"], a["lb_wqh"], a["lb_wkvh"] = x["L0_attn_b_wqkv_l"], x["L0_attn_b_wq_h"], x["L0_attn_b_wkv_h"]
    a["lb_woh"], a["lb_wol"] = x["L0_attn_b_wo_h"], x["L0_attn_b_wo_l"]
    a["lb_lng"], a["lb_lnb"], a["lb_gamma"] = x["L0_attn_b_ln_g"], x["L0_attn_b_ln_b"], x["L0_attn_b_gamma_h"]
    a["lb_rt"] = np.stack([x["L0_attn_b_rt_q"], x["L0_attn_b_rt_kv"]])
    a["lb_iota"] = np.arange(LB_SEL, dtype=f)
    a["lb_place"] = np.arange(LB_SEL, dtype=f).reshape(LB_ST, P).T
    a["lb_hmask"] = (np.arange(P)[:, None] // LB_D == np.arange(2)[None]).astype(f) * f(LB_D ** -0.5)
    a["lb_later"] = (np.arange(P)[:, None] > np.arange(P)[None]).astype(f)
    near = abs(np.arange(P)[:, None] // LB_W - (np.arange(3 * P)[None] - P) // LB_W) <= 1
    a["lb_mask"] = np.where(near, 0, -1e30).astype(f)
    a["mb_win"] = x["L1_attn_a_W_in"].T
    a["mb_wdt"] = np.tile(x["L1_attn_a_W_dt"].T, (1, 8))
    a["mb_wb"] = np.tile(x["L1_attn_a_W_x"][:MB_N].T, (1, 8))
    a["mb_wc"] = np.tile(x["L1_attn_a_W_x"][MB_N:].T, (1, 8))
    a["mb_bdt"] = np.tile(x["L1_attn_a_b_dt"], 8)[:, None]
    a["mb_alog"] = np.tile(x["L1_attn_a_A_log"], 8)[:, None]
    a["mb_wout"] = x["L1_attn_a_W_out"].T
    a["mb_cw"] = x["L1_attn_a_conv_w"][:, 0, :]
    a["mb_cb"] = x["L1_attn_a_conv_b"]
    a["mb_d"] = x["L1_attn_a_D"]
    group = np.arange(P) // MB_N
    a["mb_group"] = (group[:, None] == np.arange(8)[None]).astype(f)
    a["mb_one"] = (group[:, None] == 0).astype(f)
    tok = np.arange(T)
    size = np.array([P >> g for g in range(MB_LV)] + [P])[group][:, None]
    mid = np.where(group[:, None] < MB_LV, size // 2, 0)
    a["mb_rf"] = (tok[None] % size == mid).astype(f)
    a["mb_rb"] = (tok[None] % size == (mid - 1) % size).astype(f)
    s, g, t = np.arange(P)[:, None, None], P >> np.arange(MB_LV)[None, :, None], np.arange(P)[None, None]
    a["mb_pairs"] = ((s // g == t // g) & (s % g < g // 2) & (t % g >= g // 2)).astype(f)
    pad = ((0, F4_IC * P - F4_I), (0, 0))
    a["f4_wg"] = np.pad(x["L1_ffn_w_gate"], pad)
    a["f4_wu"] = np.pad(x["L1_ffn_w_up"], pad)
    a["f4_wd"] = x["L1_ffn_w_down"]
    a["ab_wqk"] = cat([x["L1_attn_b_Wq"].T, x["L1_attn_b_Wk"].T], 1)
    a["ab_wv"] = x["L1_attn_b_Wv"].T
    a["ab_wo"] = x["L1_attn_b_Wo"].T
    a["ab_bqk"] = cat([x["L1_attn_b_bq"], x["L1_attn_b_bk"]])
    a["ab_bv"] = x["L1_attn_b_bv"]
    a["ab_bo"] = x["L1_attn_b_bo"][None]
    a["ab_ones"] = np.ones((1, P), f)
    a["ab_hmask"] = a["da_hmask"] * f(AB_D ** -0.5)
    cos, sin = angles(10000.0, AB_D)
    a["ab_cos"] = cat([cos, cos], 2)
    a["ab_sin"] = np.stack([-sin, sin], 2)
    return {k: np.ascontiguousarray(v) for k, v in a.items()}


def kernel(**inputs):
    import concourse.bacc as bacc
    from concourse.bass_utils import run_bass_kernel_spmd

    arrays = layout({k: np.asarray(v) for k, v in inputs.items()})
    nc = bacc.Bacc("TRN2", target_bir_lowering=False, num_devices=1)
    a = {k: nc.dram_tensor("in_" + k, v.shape, mybir.dt.from_np(v.dtype), kind="ExternalInput").ap()
         for k, v in arrays.items()}
    out = nc.dram_tensor("out", (B, T, C), F32, kind="ExternalOutput").ap()
    network(nc, a, out)
    r = run_bass_kernel_spmd(nc, [{"in_" + k: v for k, v in arrays.items()}], core_ids=[0])
    return r.results[0]["out"]
```
